# Optimizing a Trainium2 kernel written in Bass

```python
import numpy as np
import jax
import jax.numpy as jnp

def _softmax(x, axis=-1):
    return jax.nn.softmax(x, axis=axis)

def _gelu(x):
    return jax.nn.gelu(x, approximate=True)

def _silu(x):
    return jax.nn.silu(x)

def _sigmoid(x):
    return jax.nn.sigmoid(x)

def _layernorm(x, axis=-1, eps=1e-05):
    m = jnp.mean(x, axis=axis, keepdims=True)
    v = jnp.var(x, axis=axis, keepdims=True)
    return (x - m) / jnp.sqrt(v + eps)

def _scatter_add(tgt, idx, src, axis=0):
    return tgt.at[idx].add(src)

def _segment_sum(src, seg, n):
    return jax.ops.segment_sum(src, seg, n)
kernel_name = 'mk_vit_tower_cls_d1_tok_img512_r4_086c2f'

def setup_inputs(seed: int=0):
    np.random.seed(seed)
    _w = jnp.asarray

    def _rec_inputs():
        import jax
        import jax.numpy as jnp
        _rk = jax.random.key(seed)
        x = -0.000190493 + 0.999948 * jax.random.normal(jax.random.fold_in(_rk, 1), (64, 2, 104, 104), jnp.float32)
        cls_tok = 0.02 * jax.random.normal(jax.random.fold_in(_rk, 5), (1, 1, 128), jnp.float32)
        return (x, cls_tok)
    x, cls_tok = _rec_inputs()

    def _L0_tok_setup():
        import jax, jax.numpy as jnp
        import numpy as np
        HP = 4
        PATCH = 8
        EPS = 1e-07

        def _shifts(x):
            h, w = (x.shape[2], x.shape[3])
            pad2 = ((0, 0), (0, 0))
            left_up = jnp.pad(x[:, :, HP:, :w - HP], pad2 + ((0, HP), (HP, 0)))
            right_up = jnp.pad(x[:, :, HP:, HP:], pad2 + ((0, HP), (0, HP)))
            left_down = jnp.pad(x[:, :, :h - HP, :w - HP], pad2 + ((HP, 0), (HP, 0)))
            right_down = jnp.pad(x[:, :, :h - HP, HP:], pad2 + ((HP, 0), (0, HP)))
            return (left_up, right_up, left_down, right_down)
        key = jax.random.key(seed)
        k1, k2, k3, k4 = jax.random.split(key, 4)
        B, C, S = (128, 2, 104)
        embed_dim = 128
        x = jax.random.normal(k1, (B, C, S, S), dtype=jnp.float32)
        gamma = 1.0 + 0.05 * jax.random.normal(k2, (10, S, S), dtype=jnp.float32)
        beta = 0.05 * jax.random.normal(k3, (10, S, S), dtype=jnp.float32)
        W = 0.02 * jax.random.normal(k4, (embed_dim, 10, PATCH, PATCH), dtype=jnp.float32)
        b = jnp.zeros((embed_dim,), dtype=jnp.float32)
        return {'x': x, 'gamma': gamma, 'beta': beta, 'W': W, 'b': b}
    _L0_tok_all = _L0_tok_setup()
    _L0_tok_in = {k: v for k, v in _L0_tok_all.items() if k in ('gamma', 'beta', 'W', 'b')}
    del _L0_tok_all

    def _L0_attn_setup():
        import jax, jax.numpy as jnp
        import numpy as np
        from jax import lax
        B, T, D = (16, 1024, 128)
        LR = 0.01
        key = jax.random.key(seed)
        k1, k2, k3, k4 = jax.random.split(key, 4)
        scale = 1.0 / jnp.sqrt(jnp.float32(D))
        return {'x': jax.random.normal(k1, (B, T, D), dtype=jnp.float32), 'Wq': jax.random.normal(k2, (D, D), dtype=jnp.float32) * scale, 'Wk': jax.random.normal(k3, (D, D), dtype=jnp.float32) * scale, 'Wv': jax.random.normal(k4, (D, D), dtype=jnp.float32) * scale, 'memory0': jnp.zeros((D, D), dtype=jnp.float32)}
    _L0_attn_all = _L0_attn_setup()
    _L0_attn_in = {k: v for k, v in _L0_attn_all.items() if k in ('Wq', 'Wk', 'Wv', 'memory0')}
    del _L0_attn_all

    def _L0_ffn_setup():
        import jax, jax.numpy as jnp
        import numpy as np
        MARK_AX = 0
        OP_MUL = 1
        OPCODE_BASE = 2
        ALU_LO, ALU_HI = (64, 80)
        AX_CARRY_LO, AX_CARRY_HI = (96, 112)
        OUTPUT_LO, OUTPUT_HI = (128, 144)
        NIB_A, NIB_B, RESULT, OP_START = (0, 1, 2, 3)
        GE_DIM = 160
        N_POS = 8
        N_LAYERS = 7
        OPCODE = 27

        def _decode_nibble(x16):
            return jnp.argmax(x16 > 0.5, axis=-1).astype(x16.dtype)
        key = jax.random.key(seed)
        k1, k2, k3 = jax.random.split(key, 3)
        x_bd = jax.random.uniform(k1, (4, 2048, 128), dtype=jnp.float32)
        W = jax.random.normal(k2, (N_LAYERS, GE_DIM, GE_DIM), dtype=jnp.float32) * 0.05
        b = jax.random.normal(k3, (N_LAYERS, GE_DIM), dtype=jnp.float32) * 0.01
        return {'x_bd': x_bd, 'W': W, 'b': b}
    _L0_ffn_all = _L0_ffn_setup()
    _L0_ffn_in = {k: v for k, v in _L0_ffn_all.items() if k in ('W', 'b')}
    del _L0_ffn_all
    return {'x': x, 'cls_tok': cls_tok, 'L0_tok_gamma': _L0_tok_in['gamma'], 'L0_tok_beta': _L0_tok_in['beta'], 'L0_tok_W': _L0_tok_in['W'], 'L0_tok_b': _L0_tok_in['b'], 'L0_attn_Wq': _L0_attn_in['Wq'], 'L0_attn_Wk': _L0_attn_in['Wk'], 'L0_attn_Wv': _L0_attn_in['Wv'], 'L0_attn_memory0': _L0_attn_in['memory0'], 'L0_ffn_W': _L0_ffn_in['W'], 'L0_ffn_b': _L0_ffn_in['b']}

def reference(x, cls_tok, L0_tok_gamma, L0_tok_beta, L0_tok_W, L0_tok_b, L0_attn_Wq, L0_attn_Wk, L0_attn_Wv, L0_attn_memory0, L0_ffn_W, L0_ffn_b):
    import jax
    import jax.numpy as jnp

    def _L0_tok_ref(x, gamma, beta, W, b):
        import jax, jax.numpy as jnp
        import numpy as np
        HP = 4
        PATCH = 8
        EPS = 1e-07

        def _shifts(x):
            h, w = (x.shape[2], x.shape[3])
            pad2 = ((0, 0), (0, 0))
            left_up = jnp.pad(x[:, :, HP:, :w - HP], pad2 + ((0, HP), (HP, 0)))
            right_up = jnp.pad(x[:, :, HP:, HP:], pad2 + ((0, HP), (0, HP)))
            left_down = jnp.pad(x[:, :, :h - HP, :w - HP], pad2 + ((HP, 0), (HP, 0)))
            right_down = jnp.pad(x[:, :, :h - HP, HP:], pad2 + ((HP, 0), (0, HP)))
            return (left_up, right_up, left_down, right_down)
        lu, ru, ld, rd = _shifts(x)
        concat = jnp.concatenate((x, lu, ru, ld, rd), axis=1)
        mean = jnp.mean(concat, axis=(1, 2, 3), keepdims=True)
        var = jnp.var(concat, axis=(1, 2, 3), keepdims=True)
        normed = (concat - mean) * jax.lax.rsqrt(var + EPS)
        normed = normed * gamma[None] + beta[None]
        y = jax.lax.conv_general_dilated(normed, W, window_strides=(PATCH, PATCH), padding='VALID', dimension_numbers=('NCHW', 'OIHW', 'NCHW'))
        y = y + b[None, :, None, None]
        B, E = (y.shape[0], y.shape[1])
        y = y.reshape(B, E, -1).transpose(0, 2, 1)
        return y

    def _L0_attn_ref(x, Wq, Wk, Wv, memory0):
        import jax, jax.numpy as jnp
        import numpy as np
        from jax import lax
        B, T, D = (16, 1024, 128)
        LR = 0.01
        q = jnp.einsum('btd,ed->bte', x, Wq)
        k = jnp.einsum('btd,ed->bte', x, Wk)
        v = jnp.einsum('btd,ed->bte', x, Wv)
        qT = jnp.swapaxes(q, 0, 1)
        kT = jnp.swapaxes(k, 0, 1)
        vT = jnp.swapaxes(v, 0, 1)

        def step(S, qkv):
            qt, kt, vt = qkv
            S = S + LR * jnp.einsum('bd,be->de', vt, kt)
            out = jnp.einsum('de,be->bd', S, qt)
            return (S, out)
        _, outs = lax.scan(step, memory0, (qT, kT, vT))
        return jnp.swapaxes(outs, 0, 1)

    def _L0_ffn_ref(x_bd, W, b):
        import jax, jax.numpy as jnp
        import numpy as np
        MARK_AX = 0
        OP_MUL = 1
        OPCODE_BASE = 2
        ALU_LO, ALU_HI = (64, 80)
        AX_CARRY_LO, AX_CARRY_HI = (96, 112)
        OUTPUT_LO, OUTPUT_HI = (128, 144)
        NIB_A, NIB_B, RESULT, OP_START = (0, 1, 2, 3)
        GE_DIM = 160
        N_POS = 8
        N_LAYERS = 7
        OPCODE = 27

        def _decode_nibble(x16):
            return jnp.argmax(x16 > 0.5, axis=-1).astype(x16.dtype)
        B, S, D = x_bd.shape
        mask = (x_bd[..., MARK_AX] >= 0.5) & (x_bd[..., OP_MUL] >= 0.5)
        a_lo = _decode_nibble(x_bd[..., ALU_LO:ALU_LO + 16])
        a_hi = _decode_nibble(x_bd[..., ALU_HI:ALU_HI + 16])
        b_lo = _decode_nibble(x_bd[..., AX_CARRY_LO:AX_CARRY_LO + 16])
        b_hi = _decode_nibble(x_bd[..., AX_CARRY_HI:AX_CARRY_HI + 16])
        op_val = x_bd[..., OPCODE_BASE + OPCODE]
        x_ge = jnp.zeros((B, S, N_POS, GE_DIM), dtype=x_bd.dtype)
        x_ge = x_ge.at[..., 0, NIB_A].set(a_lo)
        x_ge = x_ge.at[..., 1, NIB_A].set(a_hi)
        x_ge = x_ge.at[..., 0, NIB_B].set(b_lo)
        x_ge = x_ge.at[..., 1, NIB_B].set(b_hi)
        x_ge = x_ge.at[..., :, OP_START + OPCODE].set(op_val[..., None])
        h = x_ge
        for i in range(N_LAYERS):
            h = jnp.einsum('bspd,ed->bspe', h, W[i]) + b[i]
            if i < N_LAYERS - 1:
                h = jax.nn.relu(h)
        res_lo = jnp.clip(jnp.round(h[..., 0, RESULT]), 0, 15).astype(jnp.int32)
        res_hi = jnp.clip(jnp.round(h[..., 1, RESULT]), 0, 15).astype(jnp.int32)
        m = mask[..., None].astype(x_bd.dtype)
        add_lo = 2.0 * jax.nn.one_hot(res_lo, 16, dtype=x_bd.dtype) * m
        add_hi = 2.0 * jax.nn.one_hot(res_hi, 16, dtype=x_bd.dtype) * m
        out = x_bd.at[..., OUTPUT_LO:OUTPUT_LO + 16].add(add_lo)
        out = out.at[..., OUTPUT_HI:OUTPUT_HI + 16].add(add_hi)
        return out
    h = _L0_tok_ref(x, L0_tok_gamma, L0_tok_beta, L0_tok_W, L0_tok_b)
    h = jnp.concatenate([jnp.broadcast_to(cls_tok, (h.shape[0], 1, h.shape[2])), h], axis=1)
    h = h + _L0_attn_ref(_layernorm(h, axis=-1), L0_attn_Wq, L0_attn_Wk, L0_attn_Wv, L0_attn_memory0)
    h = h + _L0_ffn_ref(_layernorm(h, axis=-1), L0_ffn_W, L0_ffn_b)
    return h

_drawn_inputs = setup_inputs


def setup_inputs(seed=0):
    import zlib

    import numpy as np

    out = dict(_drawn_inputs(seed))
    spreads = {'L0_tok_b': (0.0, 0.1), 'L0_attn_memory0': (0.0, 0.527)}
    factors = {}
    for name, (base, spread) in spreads.items():
        noise = np.random.default_rng([zlib.crc32(name.encode()), seed]).standard_normal(out[name].shape)
        drawn = base * np.exp(spread * noise) if base else spread * noise
        out[name] = jnp.asarray(drawn.astype(out[name].dtype))
    for name, factor in factors.items():
        out[name] = (out[name] * factor).astype(out[name].dtype)
    return out
```

```python
from contextlib import ExitStack

import concourse.bass as bass
from concourse import mybir

F32 = mybir.dt.float32
BF16 = mybir.dt.bfloat16
ALU = mybir.AluOpType
ACT = mybir.ActivationFunctionType
AX = mybir.AxisListType

P = 128
B = 64
E = 128
S = 104
HALF = 4
N = S // (2 * HALF)
PATCHES = N * N
SHIFTS = 5
LR = 0.01
LN_EPS = 1e-5
TOK_EPS = 1e-7
PIXELS = 2 * SHIFTS * S * S

TILES = N
TOKENS = 2 * N
BODIES = N // 2
GROUPS = [range(0, 4), range(4, 7), range(7, 10), range(10, 13)]
TAIL_GROUPS = [range(0, 4), range(4, 7)]
NG = len(GROUPS)
HALF_TILE = N // 2
CLS = TILES - 1
THIRD = [0, 1, 2, 0, 1, 2, 0, 1, 2, 0, 1, 2, 1]

STAT_CHUNKS = [(0, 28), (28, 24), (52, 24), (76, 16), (92, 12)]
STATS = [(0, 4, "mid", 3), (100, 4, "mid", 3), (0, 4, "edge", 2), (100, 4, "edge", 2),
         (4, 48, "edge", 3), (52, 48, "edge", 3)] + [(4 * q, 4, "mid", 5) for q in range(1, 25)]

VECTOR_SHIFTS = {0: [0, 1], 1: [2], 2: [0, 1, 2]}
POOL_SHIFTS = {0: [3], 1: [4], 2: [3, 4]}
PARTS = 3
TERM_ROWS = PARTS * PARTS * 4
SMALLS = 16 * 6


def fixed(r, value):
    return isinstance(r, int) and r == value


def tower(nc, x_rows, x_win, gamma, beta, weight, bias, cls_tok, wq, wk, wv_t, mem_t, ident, same_image, out, parked):
    with ExitStack() as ctx:
        def sb(name, shape, dtype=F32):
            return ctx.enter_context(nc.sbuf_tensor(name, shape, dtype))

        def pb(name):
            return ctx.enter_context(nc.psum_tensor(name, [P, 512], F32))

        def sem(name):
            return ctx.enter_context(nc.semaphore(name))

        images = sb("images", [P, S, S])
        patch_rows = sb("patch_rows", [P, 2, N, B])
        offset_rows = sb("offset_rows", [P, 4, N + 1, B])
        gam = sb("gam", [P, SHIFTS, PATCHES])
        bet = sb("bet", [P, SHIFTS, PATCHES])
        wt = sb("wt", [P, SHIFTS, E])
        scaled = sb("scaled", [P, SHIFTS, TOKENS, B])
        terms = sb("terms", [TERM_ROWS, PATCHES // 2 + 1, E], BF16)
        term_rows = sb("term_rows", [P, 2, 2, E])
        term_rest = sb("term_rest", [P, 2, 2, E])
        term_parts = sb("term_parts", [P, 2, PARTS, 2, E], BF16)
        scale_rows = sb("scale_rows", [TERM_ROWS, P], BF16)
        scale_cols = sb("scale_cols", [P, 2, 2])
        scale_rest = sb("scale_rest", [P, 2, 2])
        scale_parts = sb("scale_parts", [P, 2, PARTS, PARTS, 2], BF16)
        ident_bf = sb("ident_bf", [P, P], BF16)
        bias_row = sb("bias_row", [P, E])
        ones = sb("ones", [P, P])
        wq_sb = sb("wq_sb", [P, E])
        wk_sb = sb("wk_sb", [P, E])
        wv_sb = sb("wv_sb", [P, E])
        mem_sb = sb("mem_sb", [P, E])
        ident_sb = sb("ident_sb", [P, P])
        same_sb = sb("same_sb", [P, P])
        w_vr = sb("w_vr", [P, 2 * E])
        stats = sb("stats", [P, 2 * len(STATS), 3])
        stat_w = sb("stat_w", [P, 2, 2 * len(STATS)])
        stat_tmp = sb("stat_tmp", [P, 3, 2 * len(STATS)])
        sums = sb("sums", [P, 2])
        moments = sb("moments", [P, 6])
        powers = sb("powers", [P, 5])
        h = sb("h", [P, TILES, E])
        x_hat = sb("x_hat", [P, TILES, E])
        x_hat_t = sb("x_hat_t", [P, TILES, P])
        vr = sb("vr", [P, 3, 2 * E])
        state = sb("state", [P, 2, E])
        h2 = sb("h2", [P, TILES, E])
        result = sb("result", [P, TILES, E])
        ln1_stats = sb("ln1_stats", [P, TILES, 6])
        ln1_mv = sb("ln1_mv", [P, TILES, 2])
        ln1_var = sb("ln1_var", [P, TILES])
        ln1_rstd = sb("ln1_rstd", [P, TILES])
        ln2_stats = sb("ln2_stats", [P, TILES, 6])
        ln2_mv = sb("ln2_mv", [P, TILES, 2])
        ln2_var = sb("ln2_var", [P, TILES])
        ln2_rstd = sb("ln2_rstd", [P, TILES])
        ln2_gain = sb("ln2_gain", [P, TILES])
        ln2_shift = sb("ln2_shift", [P, TILES])

        conv_ps = [pb("conv0"), pb("conv1")]
        turn_ps = pb("turn")
        vr_ps = pb("vr_ps")
        state_ps = pb("state_ps")
        out_ps = [pb("out0"), pb("out1"), pb("out2")]

        images_in = [sem(f"images_in{i}") for i in range(len(STAT_CHUNKS))]
        patch_in = [sem("patch_in_even"), sem("patch_in_odd")]
        first_offsets_in = sem("first_offsets_in")
        offset_in = [sem("offset_in_even"), sem("offset_in_odd")]
        gamma_in = sem("gamma_in")
        tables_in = sem("tables_in")
        small_in = sem("small_in")
        cls_in = sem("cls_in")
        bias_in = sem("bias_in")
        terms_parked = sem("terms_parked")
        terms_in = sem("terms_in")
        stored = [sem(f"stored{i}") for i in range(NG)]
        pads_ready = sem("pads_ready")
        bias_zero = sem("bias_zero")
        cols_zero = sem("cols_zero")
        consts_ready = sem("consts_ready")
        terms_done = sem("terms_done")
        term_rows_ready = sem("term_rows_ready")
        term_step = sem("term_step")
        term_parts_ready = sem("term_parts_ready")
        ident_bf_ready = sem("ident_bf_ready")
        product_done = sem("product_done")
        w_vr_ready = sem("w_vr_ready")
        stats_step = sem("stats_step")
        sums_ready = sem("sums_ready")
        image_sums_done = sem("image_sums_done")
        image_var_ready = sem("image_var_ready")
        image_scale_ready = sem("image_scale_ready")
        cols_ready = sem("cols_ready")
        scales_done = sem("scales_done")
        scale_rest_ready = sem("scale_rest_ready")
        scale_parts_ready = sem("scale_parts_ready")
        scale_rows_ready = sem("scale_rows_ready")
        scaled_vector = sem("scaled_vector")
        scaled_pool = sem("scaled_pool")
        last_pad = sem("last_pad")
        conv_done = sem("conv_done")
        h_ready = sem("h_ready")
        cls_stats_ready = sem("cls_stats_ready")
        mv_ready = sem("mv_ready")
        ln1_var_ready = sem("ln1_var_ready")
        ln1_rstd_ready = sem("ln1_rstd_ready")
        x_hat_ready = sem("x_hat_ready")
        turned = sem("turned")
        x_hat_t_ready = sem("x_hat_t_ready")
        vr_done = sem("vr_done")
        vr_ready = sem("vr_ready")
        state_done = sem("state_done")
        state_ready = sem("state_ready")
        out_done = sem("out_done")
        h2_ready = sem("h2_ready")
        first_stats_ready = sem("first_stats_ready")
        last_stats_ready = sem("last_stats_ready")
        ln2_var_ready = sem("ln2_var_ready")
        ln2_rstd_ready = sem("ln2_rstd_ready")
        ln2_affine_ready = sem("ln2_affine_ready")
        result_ready = sem("result_ready")

        def group_no(r, n):
            return NG * r + (n + 1)

        def tile_no(r, k):
            return TILES * r + (k + 1)

        def token_no(r, k, half):
            return TOKENS * r + (2 * k + half + 1)

        def tiles_of(r, n):
            return (TAIL_GROUPS if fixed(r, BODIES) else GROUPS)[n]

        def rows_of(r, k):
            return B if fixed(r, BODIES) and k == HALF_TILE else P

        def parts(r, n):
            tiles = tiles_of(r, n)
            if rows_of(r, tiles[-1]) == B:
                return [(tiles[0], len(tiles) - 1, P), (tiles[-1], 1, B)]
            return [(tiles[0], len(tiles), P)]

        def scaled_rows(r, k):
            return 2 * r + (1 if 2 * k + 1 < N or rows_of(r, k) == B else 2)

        def next_group(r, n, ahead):
            n += ahead
            if n >= NG and not fixed(r, BODIES):
                r, n = r + 1, n - NG
            return None if fixed(r, BODIES) and n >= len(TAIL_GROUPS) else (r, n)

        block = ctx.enter_context(nc.Block())

        @block.sync
        def _(sp):
            def load_patch_row(i, slot):
                sp.dma_start(patch_rows[:, slot], x_win[:, i]).then_inc(patch_in[slot], 16)

            def load_offset_row(i, slot, landed, upper=True, lower=True):
                for a in range(2):
                    if (upper, lower)[a]:
                        for b in range(2):
                            q, src = 32 * (2 * a + b), 32 * (2 * (1 - a) + (1 - b))
                            sp.dma_start(offset_rows[q:q + 32, slot, 1 - b:1 - b + N],
                                         x_win[src:src + 32, i - 1 + a]).then_inc(landed, 16)

            def store(r, n):
                for half in range(2):
                    for k0, count, rows in parts(r, n):
                        if rows == P or not half:
                            sp.dma_start(out[:, bass.ds(token_no(r, k0, half), count, 2)],
                                         result[half * B:half * B + B, k0:k0 + count]).then_inc(stored[n], 16)

            sp.dma_start(gam[:], gamma).then_inc(gamma_in, 16)
            load_patch_row(0, 0)
            sp.wait_ge(pads_ready, 1)
            load_offset_row(0, 0, first_offsets_in, upper=False)
            load_offset_row(1, 1, first_offsets_in)
            sp.dma_start(wt[:], weight).then_inc(tables_in, 16)
            sp.dma_start(bet[:], beta).then_inc(tables_in, 16)
            load_offset_row(2, 2, offset_in[0])
            load_patch_row(1, 1)
            for i, (row, rows) in enumerate(STAT_CHUNKS):
                sp.dma_start(images[:, row:row + rows], x_rows[:, row:row + rows]).then_inc(images_in[i], 16)

            for blk in range(2):
                sp.wait_ge(term_parts_ready, blk + 1)
                count = P if blk == 0 else PATCHES - P
                sp.dma_start(parked[:, blk * P:blk * P + count].rearrange("k p e -> p k e"),
                             term_parts[0:count, blk].rearrange("p a k e -> p (a k) e")).then_inc(terms_parked, 16)
            sp.wait_ge(consts_ready, 1)
            sp.wait_ge(terms_parked, 32)
            for i in range(2 * PARTS):
                half, row = i // PARTS, 2 * PARTS * i
                m = (PATCHES + 1 - half) // 2
                sp.dma_start(terms[row:row + 2 * PARTS, 0:m], parked[:, half:PATCHES:2]).then_inc(terms_in, 16)
            load_offset_row(3, 3, offset_in[1])

            def body(r, patch_count=2, offsets=((True, True), (True, True))):
                for half in range(len(offsets)):
                    sp.wait_ge(offset_in[half], 64 * (r + 1))
                sp.wait_ge(scaled_vector, 2 * r + 2)
                sp.wait_ge(scaled_pool, 2 * r + 2)
                for half in range(patch_count):
                    load_patch_row(2 * r + (2 + half), half)
                for half, (upper, lower) in enumerate(offsets):
                    load_offset_row(2 * r + (4 + half), 2 * (r & 1) + half, offset_in[half], upper, lower)
                if fixed(r, 0):
                    sp.wait_ge(result_ready, 1)
                    sp.dma_start(out[:, 0], result[0:B, CLS]).then_inc(stored[NG - 1], 16)
                else:
                    sp.wait_ge(result_ready, group_no(r - 1, NG - 1) + 1)
                    store(r - 1, NG - 1)
                for n in range(NG - 1):
                    sp.wait_ge(result_ready, group_no(r, n) + 1)
                    store(r, n)

            body(0)
            with sp.Fori(1, BODIES - 2) as r:
                body(r)
            body(BODIES - 2, 2, ((True, True), (True, False)))
            body(BODIES - 1, 1, ())
            for r, n in ((BODIES - 1, NG - 1), (BODIES, 0), (BODIES, 1)):
                sp.wait_ge(result_ready, group_no(r, n) + 1)
                store(r, n)
            for n in range(NG):
                sp.wait_ge(stored[n], 32 * BODIES + (32, 48, 0, 16)[n])

        @block.tensor
        def _(pe):
            def conv(r, n, a, b):
                tiles, ps = tiles_of(r, n), conv_ps[n % 2]
                for i in range(a, min(b, SHIFTS * len(tiles))):
                    k, s = tiles[i // SHIFTS], i % SHIFTS
                    at, rows = (k - tiles[0]) * E, rows_of(r, k)
                    if s == 0:
                        pe.wait_ge(scaled_vector, scaled_rows(r, k))
                        pe.wait_ge(scaled_pool, scaled_rows(r, k))
                    pe.matmul(ps[0:rows, at:at + E], scaled[:, s, 2 * k:2 * k + rows // B], wt[:, s],
                              start=(i == 0), stop=False, skip_group_check=True)
                if b > SHIFTS * len(tiles):
                    for k0, count, rows in parts(r, n):
                        at = (k0 - tiles[0]) * E
                        last = pe.matmul(ps[0:rows, at:at + count * E], scale_rows[:, 0:rows],
                                         terms[:, bass.ds(TILES * r + k0, count)],
                                         start=False, stop=True, skip_group_check=True)
                    last.then_inc(conv_done, 1)

            def turn(r, n):
                pe.wait_ge(x_hat_ready, group_no(r, n) + 1)
                pe.wait_ge(x_hat_t_ready, group_no(r, n))
                tiles = tiles_of(r, n)
                for k in tiles:
                    at, rows = (k - tiles[0]) * P, rows_of(r, k)
                    last = pe.transpose(turn_ps[:, at:at + rows], x_hat[0:rows, k], ident_sb[0:rows, 0:rows])
                last.then_inc(turned, 1)

            def values(r, n, k):
                pe.wait_ge(x_hat_t_ready, group_no(r, n) + 1)
                pe.wait_ge(vr_ready, tile_no(r, k))
                rows = rows_of(r, k)
                pe.matmul(vr_ps[0:rows, 0:2 * E], x_hat_t[:, k, 0:rows], w_vr[:], start=True,
                          stop=True).then_inc(vr_done, 1)

            def update(r, k, half):
                base = half * B
                pe.wait_ge(vr_ready, tile_no(r, k) + 1)
                pe.wait_ge(state_ready, token_no(r, k, half))
                pe.matmul(state_ps[:, 0:E], vr[base:base + B, THIRD[k], E:2 * E],
                          vr[base:base + B, THIRD[k], 0:E], start=False, stop=False,
                          skip_group_check=True).then_inc(state_done, 1)

            def read(r, k, half):
                base = half * B
                pe.wait_ge(state_ready, token_no(r, k, half) + 1)
                if half == 0 and k > 0:
                    pe.wait_ge(h2_ready, tile_no(r, k) - 1)
                last = pe.matmul(out_ps[THIRD[k]][base:base + B, 0:E], x_hat_t[:, k, base:base + B],
                                 state[:, half], start=True, stop=True)
                if half == 1 or rows_of(r, k) == B:
                    last.then_inc(out_done, 1)

            def step(r, n):
                tiles = tiles_of(r, n)
                ahead, after = next_group(r, n, 2), next_group(r, n, 1)
                total = SHIFTS * len(tiles_of(*ahead)) + 1 if ahead else 0

                def conv_share(j):
                    if ahead:
                        if j == 0:
                            pe.wait_ge(h_ready, group_no(*ahead) - 2)
                        conv(*ahead, total * j // (2 * len(tiles)), total * (j + 1) // (2 * len(tiles)))

                for i, k in enumerate(tiles):
                    update(r, k, 0)
                    if after and k == tiles[-1]:
                        turn(*after)
                    conv_share(2 * i)
                    if k != tiles[-1]:
                        values(r, n, k + 1)
                    read(r, k, 0)
                    if rows_of(r, k) == P:
                        update(r, k, 1)
                        if after and k == tiles[-1]:
                            values(*after, tiles_of(*after)[0])
                        conv_share(2 * i + 1)
                        read(r, k, 1)

            pe.wait_ge(gamma_in, 16)
            pe.wait_ge(tables_in, 32)
            pe.wait_ge(consts_ready, 1)
            pe.wait_ge(bias_in, 16)
            for blk in range(2):
                count = P if blk == 0 else PATCHES - P
                for kind, table in enumerate((bet, gam)):
                    for s in range(SHIFTS):
                        last = pe.matmul(out_ps[blk][0:count, kind * E:kind * E + E],
                                         table[:, s, blk * P:blk * P + count], wt[:, s],
                                         start=(s == 0), stop=(kind == 1 and s == SHIFTS - 1))
                    if kind == 0:
                        last = pe.matmul(out_ps[blk][0:count, 0:E], ones[:, 0:count], bias_row[:],
                                         start=False, stop=True)
                last.then_inc(terms_done, 1)
            pe.wait_ge(small_in, SMALLS)
            pe.matmul(vr_ps[:, 0:E], wk_sb[:], wq_sb[:], start=True, stop=True).then_inc(product_done, 1)
            pe.matmul(state_ps[:, 0:E], wq_sb[:], mem_sb[:], start=True, stop=False, skip_group_check=True)
            pe.wait_ge(x_hat_ready, 1)
            pe.transpose(turn_ps[:, 0:B], x_hat[0:B, CLS], ident_sb[0:B, 0:B]).then_inc(turned, 1)
            pe.wait_ge(x_hat_t_ready, 1)
            pe.wait_ge(w_vr_ready, 2)
            pe.matmul(vr_ps[0:B, 0:2 * E], x_hat_t[:, CLS, 0:B], w_vr[:], start=True,
                      stop=True).then_inc(vr_done, 1)
            conv(0, 0, 0, SHIFTS * len(GROUPS[0]))
            pe.wait_ge(vr_ready, 1)
            pe.matmul(state_ps[:, 0:E], vr[0:B, THIRD[CLS], E:2 * E], vr[0:B, THIRD[CLS], 0:E], start=False,
                      stop=False, skip_group_check=True).then_inc(state_done, 1)
            pe.wait_ge(state_ready, 1)
            pe.wait_ge(term_rows_ready, 2)
            pe.matmul(out_ps[THIRD[CLS]][0:B, 0:E], x_hat_t[:, CLS, 0:B], state[:, 1], start=True,
                      stop=True).then_inc(out_done, 1)
            conv(0, 1, 0, SHIFTS * len(GROUPS[1]))
            pe.wait_ge(sums_ready, 2)
            pe.matmul(out_ps[2][:, 0:2], same_sb[:], sums[:], start=True, stop=True).then_inc(image_sums_done, 1)
            pe.wait_ge(scale_parts_ready, 3)
            pe.wait_ge(ident_bf_ready, 1)
            pe.matmul(out_ps[2][0:TERM_ROWS, 128:256], scale_parts[:].rearrange("p h a b k -> p (h a b k)"),
                      ident_bf[:], start=True, stop=True).then_inc(scales_done, 1)
            pe.wait_ge(scale_rows_ready, 1)
            pe.wait_ge(terms_in, 16 * 2 * PARTS)
            for n in range(2):
                conv(0, n, SHIFTS * len(GROUPS[n]), SHIFTS * len(GROUPS[n]) + 1)
            turn(0, 0)
            values(0, 0, 0)
            with pe.Fori(0, BODIES - 1) as r:
                for n in range(NG):
                    step(r, n)
            for n in range(NG):
                step(BODIES - 1, n)
            for n in range(len(TAIL_GROUPS)):
                step(BODIES, n)

        @block.scalar
        def _(act):
            def rows_out(r, n):
                act.wait_ge(conv_done, group_no(r, n))
                first = tiles_of(r, n)[0]
                for k0, count, rows in parts(r, n):
                    at = (k0 - first) * E
                    last = act.activation(h[0:rows, k0:k0 + count], conv_ps[n % 2][0:rows, at:at + count * E],
                                          ACT.Identity, scale=moments[0:rows, 5:6])
                last.then_inc(h_ready, 1)

            def turn_out(r, n):
                act.wait_ge(turned, group_no(r, n) + 1)
                first = tiles_of(r, n)[0]
                for k0, count, rows in parts(r, n):
                    at = (k0 - first) * P
                    last = act.copy(x_hat_t[:, k0:k0 + count, 0:rows],
                                    turn_ps[:, at:at + (count - 1) * P + rows])
                last.then_inc(x_hat_t_ready, 1)

            def values_out(r, k):
                rows = rows_of(r, k)
                act.wait_ge(vr_done, tile_no(r, k) + 1)
                act.copy(vr[0:rows, THIRD[k]], vr_ps[0:rows, 0:2 * E]).then_inc(vr_ready, 1)

            def state_out(r, k, half):
                act.wait_ge(state_done, token_no(r, k, half) + 1)
                act.copy(state[:, half], state_ps[:, 0:E]).then_inc(state_ready, 1)

            def step(r, n):
                tiles = tiles_of(r, n)
                ahead, after = next_group(r, n, 2), next_group(r, n, 1)
                for k in tiles:
                    state_out(r, k, 0)
                    if k != tiles[-1]:
                        values_out(r, k + 1)
                    elif after:
                        turn_out(*after)
                    if rows_of(r, k) == P:
                        state_out(r, k, 1)
                        if after and k == tiles[-1]:
                            values_out(after[0], tiles_of(*after)[0])
                if ahead:
                    rows_out(*ahead)

            act.dma_start(h[0:B, CLS], cls_tok.partition_broadcast(B)).then_inc(cls_in, 16)
            for tile, src in ((wq_sb, wq), (wk_sb, wk), (wv_sb, wv_t), (mem_sb, mem_t), (ident_sb, ident),
                              (same_sb, same_image)):
                act.dma_start(tile[:], src).then_inc(small_in, 16)
            act.wait_ge(bias_zero, 1)
            act.dma_start(bias_row[0:1, :], bias).then_inc(bias_in, 16)
            act.wait_ge(small_in, SMALLS)
            act.mul(w_vr[:, 0:E], wv_sb[:], LR).then_inc(w_vr_ready, 1)
            for blk in range(2):
                count = P if blk == 0 else PATCHES - P
                act.wait_ge(terms_done, blk + 1)
                act.copy(term_rows[0:count, blk],
                         out_ps[blk][0:count, 0:2 * E]).then_inc(term_rows_ready, 1)
            act.copy(ident_bf[:], ident_sb[:]).then_inc(ident_bf_ready, 1)
            act.wait_ge(product_done, 1)
            act.copy(w_vr[:, E:2 * E], vr_ps[:, 0:E]).then_inc(w_vr_ready, 1)
            act.wait_ge(turned, 1)
            act.copy(x_hat_t[:, CLS, 0:B], turn_ps[:, 0:B]).then_inc(x_hat_t_ready, 1)
            act.wait_ge(vr_done, 1)
            act.copy(vr[0:B, THIRD[CLS]], vr_ps[0:B, 0:2 * E]).then_inc(vr_ready, 1)
            act.wait_ge(state_done, 1)
            act.copy(state[:, 1], state_ps[:, 0:E]).then_inc(state_ready, 1)
            act.wait_ge(scales_done, 1)
            act.copy(scale_rows[:], out_ps[2][0:TERM_ROWS, 128:256]).then_inc(scale_rows_ready, 1)
            rows_out(0, 0)
            rows_out(0, 1)
            turn_out(0, 0)
            values_out(0, 0)
            with act.Fori(0, BODIES - 1) as r:
                for n in range(NG):
                    step(r, n)
            for n in range(NG):
                step(BODIES - 1, n)
            for n in range(len(TAIL_GROUPS)):
                step(BODIES, n)

        def scale_shift(eng, s, i, parity):
            if s == 0:
                windows = patch_rows[:, parity]
            else:
                slot, right = (i + (1 if s < 3 else 0)) & 3, (s - 1) % 2
                windows = offset_rows[:, slot, right:right + N]
            gains = gam[:, s, bass.ds(i * N, N)].unsqueeze(2).to_broadcast([P, N, B])
            return eng.tensor_tensor(scaled[:, s, parity * N:parity * N + N], windows, gains, ALU.mult)

        def scale_part(eng, shares, done, r, n, j, of):
            parity = 0 if n < 2 else 1
            if n not in shares or fixed(r, BODIES) or (fixed(r, BODIES - 1) and parity):
                return
            mine = shares[n]
            part = mine[len(mine) * j // of:len(mine) * (j + 1) // of]
            if not part:
                return
            if part[0] == mine[0] and n != 1:
                last_row = fixed(r, BODIES - 1)
                eng.wait_ge(patch_in[parity], 16 * (r + 2))
                eng.wait_ge(offset_in[0], 64 * (r + (1 + parity)))
                eng.wait_ge(offset_in[1], 64 * (r + 1) - (32 if last_row else 0))
                if last_row:
                    eng.wait_ge(last_pad, 1)
                eng.wait_ge(conv_done, group_no(r, 3 if parity else 1))
            for s in part:
                last = scale_shift(eng, s, 2 * r + (2 + parity), parity)
            if n != 0 and part[-1] == mine[-1]:
                last.then_inc(done, 1)

        def before(r, n):
            if fixed(r, 0) and n == 0:
                return -1, 3, [CLS], None
            r0, n0 = (r, n - 1) if n else (r - 1, NG - 1)
            if n0 == NG - 1:
                return r0, n0, tiles_of(r0, n0), (stored[n0], 32 * r0 + 16)
            return r0, n0, tiles_of(r0, n0), None if fixed(r0, 0) else (stored[n0], 32 * r0)

        @block.vector
        def _(dve):
            def ln1_stats_of(r, n):
                dve.wait_ge(h_ready, group_no(r, n))
                for k in tiles_of(r, n):
                    rows = rows_of(r, k)
                    last = dve.bn_stats(ln1_stats[0:rows, k], h[0:rows, k])
                return last

            def ln1_moments(r, n):
                for k in tiles_of(r, n):
                    rows = rows_of(r, k)
                    last = dve.bn_aggr(ln1_mv[0:rows, k], ln1_stats[0:rows, k])
                return last

            def ln1_add_eps(r, n):
                a, z = tiles_of(r, n)[0], tiles_of(r, n)[-1] + 1
                dve.tensor_scalar(ln1_var[:, a:z], ln1_mv[:, a:z, 1], LN_EPS, None, ALU.add).then_inc(ln1_var_ready, 1)

            def normalise(r, n):
                dve.wait_ge(ln1_rstd_ready, group_no(r, n) + 1)
                for k in tiles_of(r, n):
                    rows = rows_of(r, k)
                    last = dve.tensor_scalar(x_hat[0:rows, k], h[0:rows, k], ln1_mv[0:rows, k, 0:1],
                                             ln1_rstd[0:rows, k:k + 1], ALU.subtract, ALU.mult)
                last.then_inc(x_hat_ready, 1)

            def add_out(r, n, k):
                rows = rows_of(r, k)
                dve.wait_ge(out_done, tile_no(r, k) + 1)
                dve.tensor_tensor(h2[0:rows, k], out_ps[THIRD[k]][0:rows, 0:E], h[0:rows, k],
                                  ALU.add).then_inc(h2_ready, 1)
                dve.wait_ge(h2_ready, tile_no(r, k) + 1)
                last = dve.bn_stats(ln2_stats[0:rows, k], h2[0:rows, k])
                if fixed(r, BODIES) and k == HALF_TILE:
                    last.then_inc(last_stats_ready, 1)

            def ln2_moments(r, n, tiles, _):
                for k in tiles:
                    rows = B if fixed(r, -1) else rows_of(r, k)
                    last = dve.bn_aggr(ln2_mv[0:rows, k], ln2_stats[0:rows, k])
                return last

            def ln2_add_eps(r, n, tiles, _):
                a, z, rows = tiles[0], tiles[-1] + 1, B if fixed(r, -1) else P
                dve.tensor_scalar(ln2_var[0:rows, a:z], ln2_mv[0:rows, a:z, 1], LN_EPS, None,
                                  ALU.add).then_inc(ln2_var_ready, 1)

            def ln2_result(r, n, tiles, slots_free):
                group, rows = group_no(r, n), B if fixed(r, -1) else P
                a, z = tiles[0], tiles[-1] + 1
                dve.wait_ge(ln2_rstd_ready, group + 1)
                dve.tensor_scalar(ln2_gain[0:rows, a:z], ln2_rstd[0:rows, a:z], 1.0, None, ALU.add)
                dve.scalar_tensor_tensor(ln2_shift[0:rows, a:z], ln2_mv[0:rows, a:z, 0], -1.0,
                                         ln2_rstd[0:rows, a:z], ALU.mult, ALU.mult).then_inc(ln2_affine_ready, 1)
                dve.wait_ge(ln2_affine_ready, group + 1)
                if slots_free:
                    dve.wait_ge(*slots_free)
                for k in tiles:
                    m = min(rows, rows_of(r, k))
                    last = dve.tensor_scalar(result[0:m, k], h2[0:m, k], ln2_gain[0:m, k:k + 1],
                                             ln2_shift[0:m, k:k + 1], ALU.mult, ALU.add)
                last.then_inc(result_ready, 1)

            def step(r, n):
                tiles, after, prev = tiles_of(r, n), next_group(r, n, 1), before(r, n)
                if after:
                    ln1_stats_of(*after)
                scale_part(dve, VECTOR_SHIFTS, scaled_vector, r, n, 0, 3)
                add_out(r, n, tiles[0])
                if after:
                    ln1_moments(*after)
                ln2_moments(*prev).then_inc(mv_ready, 1)
                dve.wait_ge(mv_ready, group_no(r, n) + 2)
                if after:
                    ln1_add_eps(*after)
                ln2_add_eps(*prev)
                scale_part(dve, VECTOR_SHIFTS, scaled_vector, r, n, 1, 3)
                if after:
                    normalise(*after)
                add_out(r, n, tiles[1])
                scale_part(dve, VECTOR_SHIFTS, scaled_vector, r, n, 2, 3)
                ln2_result(*prev)
                for k in tiles[2:]:
                    add_out(r, n, k)

            dve.memset(offset_rows[:, :, 0], 0.0)
            dve.memset(offset_rows[:, :, N], 0.0)
            dve.memset(offset_rows[0:B, 0, 1:N], 0.0).then_inc(pads_ready, 1)
            dve.memset(scale_cols[:], 0.0).then_inc(cols_zero, 1)
            dve.wait_ge(cls_in, 16)
            dve.bn_stats(ln1_stats[0:B, CLS], h[0:B, CLS]).then_inc(cls_stats_ready, 1)
            dve.wait_ge(cls_stats_ready, 1)
            dve.bn_aggr(ln1_mv[0:B, CLS], ln1_stats[0:B, CLS]).then_inc(mv_ready, 1)
            dve.wait_ge(mv_ready, 1)
            dve.tensor_scalar(ln1_var[0:B, CLS:CLS + 1], ln1_mv[0:B, CLS, 1:2], LN_EPS, None,
                              ALU.add).then_inc(ln1_var_ready, 1)
            dve.wait_ge(gamma_in, 16)
            dve.wait_ge(patch_in[0], 16)
            dve.wait_ge(first_offsets_in, 16 * 6)
            for s in range(3):
                last = scale_shift(dve, s, 0, 0)
            last.then_inc(scaled_vector, 1)
            dve.wait_ge(ln1_rstd_ready, 1)
            dve.tensor_scalar(x_hat[0:B, CLS], h[0:B, CLS], ln1_mv[0:B, CLS, 0:1],
                              ln1_rstd[0:B, CLS:CLS + 1], ALU.subtract, ALU.mult).then_inc(x_hat_ready, 1)
            dve.wait_ge(patch_in[1], 16)
            dve.wait_ge(offset_in[0], 64)
            for s in range(3):
                last = scale_shift(dve, s, 1, 1)
            last.then_inc(scaled_vector, 1)
            for i, (row, rows) in enumerate(STAT_CHUNKS):
                dve.wait_ge(images_in[i], 16)
                for j, (first, count, cols, _) in enumerate(STATS):
                    if row <= first + count - 1 < row + rows:
                        part = images[:, first:first + count]
                        if cols == "mid":
                            part = part[:, :, HALF:S - HALF]
                        else:
                            part = part.rearrange("p r (g q) -> p r g q", q=HALF)[:, :, 0:S // HALF:S // HALF - 1]
                        last_stats = dve.bn_stats(stats[:, 2 * j:2 * j + 2].rearrange("p a b -> p (a b)"), part)
            last_stats.then_inc(stats_step, 1)
            dve.wait_ge(stats_step, 1)
            dve.wait_ge(consts_ready, 1)
            dve.tensor_tensor(stat_tmp[:, 0], stats[:, :, 1], stat_w[:, 0], ALU.mult)
            dve.tensor_tensor(stat_tmp[:, 2], stats[:, :, 2], stat_w[:, 1], ALU.mult).then_inc(stats_step, 1)
            dve.wait_ge(stats_step, 2)
            dve.tensor_reduce(sums[:, 0:1], stat_tmp[:, 0], AX.X, ALU.add).then_inc(sums_ready, 1)
            dve.tensor_tensor(stat_tmp[:, 1], stat_tmp[:, 0], stats[:, :, 1], ALU.mult).then_inc(stats_step, 1)
            dve.wait_ge(stats_step, 3)
            dve.tensor_tensor(stat_tmp[:, 0], stat_tmp[:, 1], stat_tmp[:, 2], ALU.add).then_inc(stats_step, 1)
            dve.wait_ge(stats_step, 4)
            dve.tensor_reduce(sums[:, 1:2], stat_tmp[:, 0], AX.X, ALU.add).then_inc(sums_ready, 1)
            dve.wait_ge(image_sums_done, 1)
            dve.tensor_scalar(moments[:, 0:2], out_ps[2][:, 0:2], 1.0 / PIXELS, None, ALU.mult).then_inc(stats_step, 1)
            dve.wait_ge(stats_step, 5)
            dve.tensor_tensor(moments[:, 2:3], moments[:, 0:1], moments[:, 0:1], ALU.mult).then_inc(stats_step, 1)
            dve.wait_ge(stats_step, 6)
            dve.scalar_tensor_tensor(moments[:, 3:4], moments[:, 1:2], TOK_EPS, moments[:, 2:3], ALU.add,
                                     ALU.subtract).then_inc(image_var_ready, 1)
            dve.wait_ge(cols_zero, 1)
            for half in range(2):
                a = half * B
                dve.tensor_scalar(scale_cols[a:a + B, half, 1:2], moments[a:a + B, 0:1], -1.0, None,
                                  ALU.mult).then_inc(cols_ready, 1)
            dve.wait_ge(image_scale_ready, 1)
            for half in range(2):
                a = half * B
                dve.tensor_copy(scale_cols[a:a + B, half, 0:1], moments[a:a + B, 4:5]).then_inc(cols_ready, 1)
            def once_each(cols):
                return cols.unsqueeze(2).to_broadcast([P, 2, PARTS, 2])

            dve.wait_ge(cols_ready, 4)
            dve.tensor_copy(scale_parts[:, :, 0], once_each(scale_cols[:])).then_inc(scale_parts_ready, 1)
            dve.wait_ge(scale_parts_ready, 1)
            dve.tensor_tensor(scale_rest[:], scale_cols[:], scale_parts[:, :, 0, 0], ALU.subtract).then_inc(scale_rest_ready, 1)
            dve.wait_ge(scale_rest_ready, 1)
            dve.tensor_copy(scale_parts[:, :, 1], once_each(scale_rest[:])).then_inc(scale_parts_ready, 1)
            dve.wait_ge(scale_parts_ready, 2)
            dve.tensor_tensor(scale_parts[:, :, 2], once_each(scale_rest[:]), scale_parts[:, :, 1],
                              ALU.subtract).then_inc(scale_parts_ready, 1)
            dve.wait_ge(out_done, 1)
            dve.tensor_tensor(h2[0:B, CLS], out_ps[THIRD[CLS]][0:B, 0:E], h[0:B, CLS],
                              ALU.add).then_inc(h2_ready, 1)
            dve.wait_ge(h2_ready, 1)
            dve.bn_stats(ln2_stats[0:B, CLS], h2[0:B, CLS])
            ln1_stats_of(0, 0).then_inc(first_stats_ready, 1)
            dve.wait_ge(first_stats_ready, 1)
            ln1_moments(0, 0).then_inc(mv_ready, 1)
            dve.wait_ge(mv_ready, 2)
            ln1_add_eps(0, 0)
            normalise(0, 0)
            for n in range(NG):
                step(0, n)
            with dve.Fori(1, BODIES - 1) as r:
                for n in range(NG):
                    step(r, n)
            for n in range(NG):
                step(BODIES - 1, n)
            for n in range(len(TAIL_GROUPS)):
                step(BODIES, n)
            prev = before(BODIES, len(TAIL_GROUPS))
            dve.wait_ge(last_stats_ready, 1)
            ln2_moments(*prev).then_inc(mv_ready, 1)
            dve.wait_ge(mv_ready, group_no(BODIES, len(TAIL_GROUPS)) + 2)
            ln2_add_eps(*prev)
            ln2_result(*prev)

        @block.gpsimd
        def _(pool):
            def ln1_power(r, n):
                a, z = tiles_of(r, n)[0], tiles_of(r, n)[-1] + 1
                pool.wait_ge(ln1_var_ready, group_no(r, n) + 1)
                pool.tensor_tensor(ln1_rstd[:, a:z], ln1_var[:, a:z], powers[:, 1:1 + z - a],
                                   ALU.pow).then_inc(ln1_rstd_ready, 1)

            def ln2_power(r, n, tiles, _):
                a, z, rows = tiles[0], tiles[-1] + 1, B if fixed(r, -1) else P
                pool.wait_ge(ln2_var_ready, group_no(r, n) + 1)
                pool.tensor_tensor(ln2_rstd[0:rows, a:z], ln2_var[0:rows, a:z], powers[0:rows, 1:1 + z - a],
                                   ALU.pow).then_inc(ln2_rstd_ready, 1)

            def step(r, n):
                after = next_group(r, n, 1)
                scale_part(pool, POOL_SHIFTS, scaled_pool, r, n, 0, 2)
                if after:
                    ln1_power(*after)
                ln2_power(*before(r, n))
                scale_part(pool, POOL_SHIFTS, scaled_pool, r, n, 1, 2)

            pool.memset(bias_row[:], 0.0).then_inc(bias_zero, 1)
            pool.memset(powers[:, 1:5], -0.5)
            pool.memset(powers[:, 0:1], 0.5)
            pool.memset(ones[:], 1.0)
            pool.memset(terms[:, PATCHES // 2], 0.0)
            for a, z in ((0, 2), (2, 4), (4, 6), (6, len(STATS))):
                _, rows, cols, w = STATS[a]
                count = rows * (S - 2 * HALF if cols == "mid" else 2 * HALF)
                pool.memset(stat_w[:, 0, 2 * a:2 * z], float(w * count // 2))
                last = pool.memset(stat_w[:, 1, 2 * a:2 * z], float(w))
            last.then_inc(consts_ready, 1)
            pool.wait_ge(consts_ready, 1)
            pool.wait_ge(ln1_var_ready, 1)
            pool.tensor_tensor(ln1_rstd[0:B, CLS:CLS + 1], ln1_var[0:B, CLS:CLS + 1], powers[0:B, 1:2],
                               ALU.pow).then_inc(ln1_rstd_ready, 1)
            pool.wait_ge(gamma_in, 16)
            pool.wait_ge(first_offsets_in, 16 * 6)
            for s in (3, 4):
                last = scale_shift(pool, s, 0, 0)
            last.then_inc(scaled_pool, 1)
            pool.wait_ge(offset_in[0], 64)
            for s in (3, 4):
                last = scale_shift(pool, s, 1, 1)
            last.then_inc(scaled_pool, 1)
            for blk in range(2):
                m = P if blk == 0 else PATCHES - P
                parts_of, rest = term_parts[0:m, blk], term_rest[0:m, blk]
                pool.wait_ge(term_rows_ready, blk + 1)
                pool.tensor_copy(parts_of[:, 0], term_rows[0:m, blk]).then_inc(term_step, 1)
                pool.wait_ge(term_step, 3 * blk + 1)
                pool.tensor_tensor(rest, term_rows[0:m, blk], parts_of[:, 0], ALU.subtract).then_inc(term_step, 1)
                pool.wait_ge(term_step, 3 * blk + 2)
                pool.tensor_copy(parts_of[:, 1], rest).then_inc(term_step, 1)
                pool.wait_ge(term_step, 3 * blk + 3)
                pool.tensor_tensor(parts_of[:, 2], rest, parts_of[:, 1], ALU.subtract).then_inc(term_parts_ready, 1)
            pool.wait_ge(image_var_ready, 1)
            pool.tensor_tensor(moments[:, 4:6], moments[:, 3:4].to_broadcast([P, 2]), powers[:, 0:2],
                               ALU.pow).then_inc(image_scale_ready, 1)
            ln1_power(0, 0)
            for n in range(NG):
                step(0, n)
            with pool.Fori(1, BODIES - 2) as r:
                for n in range(NG):
                    step(r, n)
            pool.wait_ge(scaled_vector, 2 * (BODIES - 1))
            pool.wait_ge(scaled_pool, 2 * (BODIES - 1))
            pool.wait_ge(ln2_rstd_ready, group_no(BODIES - 3, NG - 2) + 1)
            pool.memset(offset_rows[B:P, 1], 0.0).then_inc(last_pad, 1)
            pool.wait_ge(last_pad, 1)
            for r in (BODIES - 2, BODIES - 1):
                for n in range(NG):
                    step(r, n)
            for n in range(len(TAIL_GROUPS)):
                step(BODIES, n)
            ln2_power(*before(BODIES, len(TAIL_GROUPS)))


def kernel(x, cls_tok, L0_tok_gamma, L0_tok_beta, L0_tok_W, L0_tok_b, L0_attn_Wq, L0_attn_Wk, L0_attn_Wv,
           L0_attn_memory0, L0_ffn_W, L0_ffn_b):
    import numpy as np
    import concourse.bacc as bacc
    from concourse.bass_utils import run_bass_kernel_spmd

    def windows(a):
        m = a.shape[0]
        a = a.reshape(m, 2, N, 2, HALF, N, 2, HALF)
        return a.transpose(3, 6, 1, 4, 7, 0, 2, 5).reshape(P, m, N, N)

    x, gamma, beta, w = (np.asarray(a) for a in (x, L0_tok_gamma, L0_tok_beta, L0_tok_W))
    arrays = {
        "x_rows": x.reshape(P, S, S),
        "x_win": windows(x).transpose(0, 2, 3, 1),
        "gamma": windows(gamma.reshape(SHIFTS, 2, S, S)).reshape(P, SHIFTS, PATCHES),
        "beta": windows(beta.reshape(SHIFTS, 2, S, S)).reshape(P, SHIFTS, PATCHES),
        "weight": w.reshape(E, SHIFTS, 2, 2, HALF, 2, HALF).transpose(3, 5, 2, 4, 6, 1, 0).reshape(P, SHIFTS, E),
        "bias": np.asarray(L0_tok_b).reshape(1, E),
        "cls_tok": np.asarray(cls_tok).reshape(E),
        "wq": np.asarray(L0_attn_Wq),
        "wk": np.asarray(L0_attn_Wk),
        "wv_t": np.asarray(L0_attn_Wv).T,
        "mem_t": np.asarray(L0_attn_memory0).T,
        "ident": np.eye(P, dtype=np.float32),
        "same_image": np.kron(np.eye(B, dtype=np.float32), np.ones((2, 1), np.float32))[:, list(range(B)) * 2],
    }
    nc = bacc.Bacc("TRN2", target_bir_lowering=False, num_devices=1)
    in_map, args = {}, []
    for name, a in arrays.items():
        in_map[name] = np.ascontiguousarray(a)
        args.append(nc.dram_tensor(name, in_map[name].shape, F32, kind="ExternalInput").ap())
    args.append(nc.dram_tensor("out", (B, PATCHES + 1, E), F32, kind="ExternalOutput").ap())
    args.append(nc.dram_tensor("parked", (2 * PARTS, PATCHES, E), BF16, kind="Internal").ap())
    tower(nc, *args)
    return run_bass_kernel_spmd(nc, [in_map], core_ids=[0]).results[0]["out"]
```

```python
from contextlib import ExitStack

import concourse.bass as bass
from concourse import mybir

F32 = mybir.dt.float32
BF16 = mybir.dt.bfloat16
ALU = mybir.AluOpType
ACT = mybir.ActivationFunctionType
AX = mybir.AxisListType

P = 128
B = 64
E = 128
S = 104
HALF = 4
N = S // (2 * HALF)
PATCHES = N * N
SHIFTS = 5
LR = 0.01
LN_EPS = 1e-5
TOK_EPS = 1e-7
PIXELS = 2 * SHIFTS * S * S

TILES = N
TOKENS = 2 * N
BODIES = N // 2
GROUPS = [range(0, 4), range(4, 7), range(7, 10), range(10, 13)]
TAIL_GROUPS = [range(0, 4), range(4, 7)]
NG = len(GROUPS)
HALF_TILE = N // 2
CLS = TILES - 1
THIRD = [0, 1, 2, 0, 1, 2, 0, 1, 2, 0, 1, 2, 1]

STAT_CHUNKS = [(0, 28), (28, 24), (52, 24), (76, 16), (92, 12)]
STATS = [(0, 4, "mid", 3), (100, 4, "mid", 3), (0, 4, "edge", 2), (100, 4, "edge", 2),
         (4, 48, "edge", 3), (52, 48, "edge", 3)] + [(4 * q, 4, "mid", 5) for q in range(1, 25)]

VECTOR_SHIFTS = {0: [0, 1, 2], 2: [0, 1], 3: [2]}
POOL_SHIFTS = {0: [3, 4], 2: [3], 3: [4]}
PARTS = 3
TERM_ROWS = PARTS * PARTS * 4
SMALLS = 16 * 6


def fixed(r, value):
    return isinstance(r, int) and r == value


def tower(nc, x_rows, x_win, gamma, beta, weight, bias, cls_tok, wq, wk, wv_t, mem_t, ident, same_image, out, parked):
    with ExitStack() as ctx:
        def sb(name, shape, dtype=F32):
            return ctx.enter_context(nc.sbuf_tensor(name, shape, dtype))

        def pb(name):
            return ctx.enter_context(nc.psum_tensor(name, [P, 512], F32))

        def sem(name):
            return ctx.enter_context(nc.semaphore(name))

        images = sb("images", [P, S, S])
        patch_rows = sb("patch_rows", [P, 2, N, B])
        offset_rows = sb("offset_rows", [P, 4, N + 1, B])
        gam = sb("gam", [P, SHIFTS, PATCHES])
        bet = sb("bet", [P, SHIFTS, PATCHES])
        wt = sb("wt", [P, SHIFTS, E])
        scaled = sb("scaled", [P, SHIFTS, TOKENS, B])
        terms = sb("terms", [TERM_ROWS, PATCHES // 2 + 1, E], BF16)
        term_rows = sb("term_rows", [P, 2, 2, E])
        term_rest = sb("term_rest", [P, 2, 2, E])
        term_parts = sb("term_parts", [P, 2, PARTS, 2, E], BF16)
        scale_rows = sb("scale_rows", [TERM_ROWS, P], BF16)
        scale_cols = sb("scale_cols", [P, 2, 2])
        scale_rest = sb("scale_rest", [P, 2, 2])
        scale_parts = sb("scale_parts", [P, 2, PARTS, PARTS, 2], BF16)
        ident_bf = sb("ident_bf", [P, P], BF16)
        bias_row = sb("bias_row", [P, E])
        ones = sb("ones", [P, P])
        wq_sb = sb("wq_sb", [P, E])
        wk_sb = sb("wk_sb", [P, E])
        wv_sb = sb("wv_sb", [P, E])
        mem_sb = sb("mem_sb", [P, E])
        ident_sb = sb("ident_sb", [P, P])
        same_sb = sb("same_sb", [P, P])
        w_vr = sb("w_vr", [P, 2 * E])
        stats = sb("stats", [P, 2 * len(STATS), 3])
        stat_w = sb("stat_w", [P, 2, 2 * len(STATS)])
        stat_tmp = sb("stat_tmp", [P, 3, 2 * len(STATS)])
        sums = sb("sums", [P, 2])
        moments = sb("moments", [P, 6])
        powers = sb("powers", [P, 5])
        h = sb("h", [P, TILES, E])
        x_hat = sb("x_hat", [P, TILES, E])
        x_hat_t = sb("x_hat_t", [P, TILES, P])
        vr = sb("vr", [P, 3, 2 * E])
        state = sb("state", [P, 2, E])
        h2 = sb("h2", [P, TILES, E])
        result = sb("result", [P, TILES, E])
        ln1_stats = sb("ln1_stats", [P, TILES, 6])
        ln1_mv = sb("ln1_mv", [P, TILES, 2])
        ln1_var = sb("ln1_var", [P, TILES])
        ln1_rstd = sb("ln1_rstd", [P, TILES])
        ln2_stats = sb("ln2_stats", [P, TILES, 6])
        ln2_mv = sb("ln2_mv", [P, TILES, 2])
        ln2_var = sb("ln2_var", [P, TILES])
        ln2_rstd = sb("ln2_rstd", [P, TILES])
        ln2_gain = sb("ln2_gain", [P, TILES])
        ln2_shift = sb("ln2_shift", [P, TILES])

        conv_ps = [pb("conv0"), pb("conv1")]
        turn_ps = pb("turn")
        vr_ps = pb("vr_ps")
        state_ps = pb("state_ps")
        out_ps = [pb("out0"), pb("out1"), pb("out2")]

        images_in = [sem(f"images_in{i}") for i in range(len(STAT_CHUNKS))]
        patch_in = [sem("patch_in_even"), sem("patch_in_odd")]
        first_offsets_in = sem("first_offsets_in")
        offset_in = [sem("offset_in_even"), sem("offset_in_odd")]
        gamma_in = sem("gamma_in")
        tables_in = sem("tables_in")
        small_in = sem("small_in")
        cls_in = sem("cls_in")
        bias_in = sem("bias_in")
        terms_parked = sem("terms_parked")
        terms_in = sem("terms_in")
        stored = [sem(f"stored{i}") for i in range(NG)]
        pads_ready = sem("pads_ready")
        bias_zero = sem("bias_zero")
        cols_zero = sem("cols_zero")
        consts_ready = sem("consts_ready")
        terms_done = sem("terms_done")
        term_rows_ready = sem("term_rows_ready")
        term_step = sem("term_step")
        term_parts_ready = sem("term_parts_ready")
        ident_bf_ready = sem("ident_bf_ready")
        product_done = sem("product_done")
        w_vr_ready = sem("w_vr_ready")
        stats_step = sem("stats_step")
        sums_ready = sem("sums_ready")
        image_sums_done = sem("image_sums_done")
        image_var_ready = sem("image_var_ready")
        image_scale_ready = sem("image_scale_ready")
        cols_ready = sem("cols_ready")
        scales_done = sem("scales_done")
        scale_rest_ready = sem("scale_rest_ready")
        scale_parts_ready = sem("scale_parts_ready")
        scale_rows_ready = sem("scale_rows_ready")
        scaled_vector = sem("scaled_vector")
        scaled_pool = sem("scaled_pool")
        last_pad = sem("last_pad")
        conv_done = sem("conv_done")
        raw_ready = sem("raw_ready")
        first_terms_done = sem("first_terms_done")
        first_terms_ready = sem("first_terms_ready")
        h_ready = sem("h_ready")
        cls_stats_ready = sem("cls_stats_ready")
        mv_ready = sem("mv_ready")
        ln1_var_ready = sem("ln1_var_ready")
        ln1_rstd_ready = sem("ln1_rstd_ready")
        x_hat_ready = sem("x_hat_ready")
        turned = sem("turned")
        x_hat_t_ready = sem("x_hat_t_ready")
        vr_done = sem("vr_done")
        vr_ready = sem("vr_ready")
        state_done = sem("state_done")
        state_ready = sem("state_ready")
        out_done = sem("out_done")
        h2_ready = sem("h2_ready")
        first_stats_ready = sem("first_stats_ready")
        last_stats_ready = sem("last_stats_ready")
        ln2_var_ready = sem("ln2_var_ready")
        ln2_rstd_ready = sem("ln2_rstd_ready")
        ln2_affine_ready = sem("ln2_affine_ready")
        result_ready = sem("result_ready")

        def group_no(r, n):
            return NG * r + (n + 1)

        def tile_no(r, k):
            return TILES * r + (k + 1)

        def token_no(r, k, half):
            return TOKENS * r + (2 * k + half + 1)

        def tiles_of(r, n):
            return (TAIL_GROUPS if fixed(r, BODIES) else GROUPS)[n]

        def rows_of(r, k):
            return B if fixed(r, BODIES) and k == HALF_TILE else P

        def parts(r, n):
            tiles = tiles_of(r, n)
            if rows_of(r, tiles[-1]) == B:
                return [(tiles[0], len(tiles) - 1, P), (tiles[-1], 1, B)]
            return [(tiles[0], len(tiles), P)]

        def scaled_rows(r, k):
            return 2 * r + (1 if 2 * k + 1 < N or rows_of(r, k) == B else 2)

        def next_group(r, n, ahead):
            n += ahead
            if n >= NG and not fixed(r, BODIES):
                r, n = r + 1, n - NG
            return None if fixed(r, BODIES) and n >= len(TAIL_GROUPS) else (r, n)

        block = ctx.enter_context(nc.Block())

        @block.sync
        def _(sp):
            def load_patch_row(i, slot):
                sp.dma_start(patch_rows[:, slot], x_win[:, i]).then_inc(patch_in[slot], 16)

            def load_offset_row(i, slot, landed, upper=True, lower=True):
                for a in range(2):
                    if (upper, lower)[a]:
                        for b in range(2):
                            q, src = 32 * (2 * a + b), 32 * (2 * (1 - a) + (1 - b))
                            sp.dma_start(offset_rows[q:q + 32, slot, 1 - b:1 - b + N],
                                         x_win[src:src + 32, i - 1 + a]).then_inc(landed, 16)

            def store(r, n):
                for half in range(2):
                    for k0, count, rows in parts(r, n):
                        if rows == P or not half:
                            sp.dma_start(out[:, bass.ds(token_no(r, k0, half), count, 2)],
                                         result[half * B:half * B + B, k0:k0 + count]).then_inc(stored[n], 16)

            sp.dma_start(gam[:], gamma).then_inc(gamma_in, 16)
            load_patch_row(0, 0)
            sp.wait_ge(pads_ready, 1)
            load_offset_row(0, 0, first_offsets_in, upper=False)
            load_offset_row(1, 1, first_offsets_in)
            sp.dma_start(wt[:], weight).then_inc(tables_in, 16)
            sp.dma_start(bet[:], beta).then_inc(tables_in, 16)
            load_offset_row(2, 2, offset_in[0])
            load_patch_row(1, 1)
            for i, (row, rows) in enumerate(STAT_CHUNKS):
                sp.dma_start(images[:, row:row + rows], x_rows[:, row:row + rows]).then_inc(images_in[i], 16)

            for blk in range(2):
                sp.wait_ge(term_parts_ready, blk + 1)
                count = P if blk == 0 else PATCHES - P
                sp.dma_start(parked[:, blk * P:blk * P + count].rearrange("k p e -> p k e"),
                             term_parts[0:count, blk].rearrange("p a k e -> p (a k) e")).then_inc(terms_parked, 16)
            load_offset_row(3, 3, offset_in[1])
            sp.wait_ge(scaled_vector, 1)
            sp.wait_ge(scaled_pool, 1)
            load_patch_row(2, 0)
            sp.wait_ge(consts_ready, 1)
            sp.wait_ge(terms_parked, 32)
            for i in range(2 * PARTS):
                half, row = i // PARTS, 2 * PARTS * i
                m = (PATCHES + 1 - half) // 2
                sp.dma_start(terms[row:row + 2 * PARTS, 0:m], parked[:, half:PATCHES:2]).then_inc(terms_in, 16)
            sp.wait_ge(scaled_vector, 2)
            sp.wait_ge(scaled_pool, 2)
            sp.wait_ge(offset_in[0], 64)
            load_patch_row(3, 1)
            load_offset_row(4, 0, offset_in[0])
            sp.wait_ge(offset_in[1], 64)
            load_offset_row(5, 1, offset_in[1])
            sp.wait_ge(scaled_vector, 3)
            sp.wait_ge(scaled_pool, 3)
            load_patch_row(4, 0)

            def body(r, loads=True, lower=True):
                if fixed(r, 0):
                    sp.wait_ge(result_ready, 1)
                    sp.dma_start(out[:, 0], result[0:B, CLS]).then_inc(stored[NG - 1], 16)
                else:
                    sp.wait_ge(result_ready, group_no(r - 1, NG - 1) + 1)
                    store(r - 1, NG - 1)
                if loads:
                    for half in range(2):
                        sp.wait_ge(offset_in[half], 64 * (r + 2))
                    sp.wait_ge(scaled_vector, 2 * r + 4)
                    sp.wait_ge(scaled_pool, 2 * r + 4)
                    load_patch_row(2 * r + 5, 1)
                    for half in range(2):
                        load_offset_row(2 * r + (6 + half), 2 * ((r + 1) & 1) + half, offset_in[half],
                                        lower=lower or half == 0)
                for n in range(NG - 1):
                    sp.wait_ge(result_ready, group_no(r, n) + 1)
                    store(r, n)
                if loads:
                    sp.wait_ge(scaled_vector, 2 * r + 5)
                    sp.wait_ge(scaled_pool, 2 * r + 5)
                    load_patch_row(2 * r + 6, 0)

            body(0)
            with sp.Fori(1, BODIES - 3) as r:
                body(r)
            body(BODIES - 3, lower=False)
            body(BODIES - 2, loads=False)
            body(BODIES - 1, loads=False)
            for r, n in ((BODIES - 1, NG - 1), (BODIES, 0), (BODIES, 1)):
                sp.wait_ge(result_ready, group_no(r, n) + 1)
                store(r, n)
            for n in range(NG):
                sp.wait_ge(stored[n], 32 * BODIES + (32, 48, 0, 16)[n])

        @block.tensor
        def _(pe):
            def conv(r, n, a, b):
                tiles, ps = tiles_of(r, n), conv_ps[n % 2]
                for i in range(a, min(b, SHIFTS * len(tiles))):
                    k, s = tiles[i // SHIFTS], i % SHIFTS
                    at, rows = (k - tiles[0]) * E, rows_of(r, k)
                    if s == 0:
                        pe.wait_ge(scaled_vector, scaled_rows(r, k))
                        pe.wait_ge(scaled_pool, scaled_rows(r, k))
                    pe.matmul(ps[0:rows, at:at + E], scaled[:, s, 2 * k:2 * k + rows // B], wt[:, s],
                              start=(i == 0), stop=False, skip_group_check=True)
                if b > SHIFTS * len(tiles):
                    for k0, count, rows in parts(r, n):
                        at = (k0 - tiles[0]) * E
                        last = pe.matmul(ps[0:rows, at:at + count * E], scale_rows[:, 0:rows],
                                         terms[:, bass.ds(TILES * r + k0, count)],
                                         start=False, stop=True, skip_group_check=True)
                    last.then_inc(conv_done, 1)

            def conv_early(n):
                tiles = GROUPS[n]
                for k in tiles:
                    pe.wait_ge(scaled_vector, scaled_rows(0, k))
                    pe.wait_ge(scaled_pool, scaled_rows(0, k))
                    for s in range(SHIFTS):
                        last = pe.matmul(conv_ps[n][:, (k - tiles[0]) * E:(k - tiles[0]) * E + E],
                                         scaled[:, s, 2 * k:2 * k + 2], wt[:, s], start=(k == tiles[0] and s == 0),
                                         stop=(s == SHIFTS - 1), skip_group_check=True)
                last.then_inc(conv_done, 1)

            def turn(r, n):
                pe.wait_ge(x_hat_ready, group_no(r, n) + 1)
                pe.wait_ge(x_hat_t_ready, group_no(r, n))
                tiles = tiles_of(r, n)
                for k in tiles:
                    at, rows = (k - tiles[0]) * P, rows_of(r, k)
                    last = pe.transpose(turn_ps[:, at:at + rows], x_hat[0:rows, k], ident_sb[0:rows, 0:rows])
                last.then_inc(turned, 1)

            def values(r, n, k):
                pe.wait_ge(x_hat_t_ready, group_no(r, n) + 1)
                pe.wait_ge(vr_ready, tile_no(r, k))
                rows = rows_of(r, k)
                pe.matmul(vr_ps[0:rows, 0:2 * E], x_hat_t[:, k, 0:rows], w_vr[:], start=True,
                          stop=True).then_inc(vr_done, 1)

            def update(r, k, half):
                base = half * B
                pe.wait_ge(vr_ready, tile_no(r, k) + 1)
                pe.wait_ge(state_ready, token_no(r, k, half))
                pe.matmul(state_ps[:, 0:E], vr[base:base + B, THIRD[k], E:2 * E],
                          vr[base:base + B, THIRD[k], 0:E], start=False, stop=False,
                          skip_group_check=True).then_inc(state_done, 1)

            def read(r, k, half):
                base = half * B
                pe.wait_ge(state_ready, token_no(r, k, half) + 1)
                if half == 0 and k > 0:
                    pe.wait_ge(h2_ready, tile_no(r, k) - 1)
                last = pe.matmul(out_ps[THIRD[k]][base:base + B, 0:E], x_hat_t[:, k, base:base + B],
                                 state[:, half], start=True, stop=True)
                if half == 1 or rows_of(r, k) == B:
                    last.then_inc(out_done, 1)

            def step(r, n):
                tiles = tiles_of(r, n)
                ahead, after = next_group(r, n, NG), next_group(r, n, 1)
                total = SHIFTS * len(tiles_of(*ahead)) + 1 if ahead else 0

                def conv_share(j):
                    if ahead:
                        if j == 0:
                            pe.wait_ge(h_ready, group_no(*ahead) - 2)
                        conv(*ahead, total * j // (2 * len(tiles)), total * (j + 1) // (2 * len(tiles)))

                for i, k in enumerate(tiles):
                    update(r, k, 0)
                    if after and k == tiles[-1]:
                        turn(*after)
                    conv_share(2 * i)
                    if k != tiles[-1]:
                        values(r, n, k + 1)
                    if rows_of(r, k) == P:
                        update(r, k, 1)
                        if after and k == tiles[-1]:
                            values(*after, tiles_of(*after)[0])
                        conv_share(2 * i + 1)
                    read(r, k, 0)
                    if rows_of(r, k) == P:
                        read(r, k, 1)

            pe.wait_ge(gamma_in, 16)
            pe.wait_ge(tables_in, 32)
            pe.wait_ge(consts_ready, 1)
            pe.wait_ge(bias_in, 16)
            for blk in range(2):
                count = P if blk == 0 else PATCHES - P
                for kind, table in enumerate((bet, gam)):
                    for s in range(SHIFTS):
                        last = pe.matmul(out_ps[blk][0:count, kind * E:kind * E + E],
                                         table[:, s, blk * P:blk * P + count], wt[:, s],
                                         start=(s == 0), stop=(kind == 1 and s == SHIFTS - 1))
                    if kind == 0:
                        last = pe.matmul(out_ps[blk][0:count, 0:E], ones[:, 0:count], bias_row[:],
                                         start=False, stop=True)
                last.then_inc(terms_done, 1)
            pe.wait_ge(small_in, SMALLS)
            pe.matmul(vr_ps[:, 0:E], wk_sb[:], wq_sb[:], start=True, stop=True).then_inc(product_done, 1)
            pe.matmul(state_ps[:, 0:E], wq_sb[:], mem_sb[:], start=True, stop=False, skip_group_check=True)
            pe.wait_ge(x_hat_ready, 1)
            pe.transpose(turn_ps[:, 0:B], x_hat[0:B, CLS], ident_sb[0:B, 0:B]).then_inc(turned, 1)
            pe.wait_ge(x_hat_t_ready, 1)
            pe.wait_ge(w_vr_ready, 2)
            pe.matmul(vr_ps[0:B, 0:2 * E], x_hat_t[:, CLS, 0:B], w_vr[:], start=True,
                      stop=True).then_inc(vr_done, 1)
            conv_early(0)
            pe.wait_ge(vr_ready, 1)
            pe.matmul(state_ps[:, 0:E], vr[0:B, THIRD[CLS], E:2 * E], vr[0:B, THIRD[CLS], 0:E], start=False,
                      stop=False, skip_group_check=True).then_inc(state_done, 1)
            pe.wait_ge(state_ready, 1)
            pe.wait_ge(term_rows_ready, 2)
            pe.matmul(out_ps[THIRD[CLS]][0:B, 0:E], x_hat_t[:, CLS, 0:B], state[:, 1], start=True,
                      stop=True).then_inc(out_done, 1)
            conv_early(1)
            pe.wait_ge(raw_ready, 1)
            conv(0, 2, 0, SHIFTS * len(GROUPS[2]))
            pe.wait_ge(sums_ready, 2)
            pe.matmul(out_ps[2][:, 0:2], same_sb[:], sums[:], start=True, stop=True).then_inc(image_sums_done, 1)
            pe.wait_ge(raw_ready, 2)
            meanwhile = SHIFTS * (len(GROUPS[3]) - 1)
            conv(0, 3, 0, meanwhile)
            pe.wait_ge(scale_parts_ready, 3)
            pe.wait_ge(ident_bf_ready, 1)
            pe.matmul(out_ps[2][0:TERM_ROWS, 128:256], scale_parts[:].rearrange("p h a b k -> p (h a b k)"),
                      ident_bf[:], start=True, stop=True).then_inc(scales_done, 1)
            conv(0, 3, meanwhile, SHIFTS * len(GROUPS[3]))
            pe.wait_ge(scale_rows_ready, 1)
            pe.wait_ge(terms_in, 16 * 2 * PARTS)
            for n in range(2):
                k0, count = GROUPS[n][0], len(GROUPS[n])
                pe.matmul(out_ps[2 * n][:, 0:count * E], scale_rows[:], terms[:, k0:k0 + count], start=True,
                          stop=True).then_inc(first_terms_done, 1)
            for n in range(2, NG):
                conv(0, n, SHIFTS * len(GROUPS[n]), SHIFTS * len(GROUPS[n]) + 1)
            pe.wait_ge(h_ready, 2)
            turn(0, 0)
            values(0, 0, 0)
            with pe.Fori(0, BODIES - 1) as r:
                for n in range(NG):
                    step(r, n)
            for n in range(NG):
                step(BODIES - 1, n)
            for n in range(len(TAIL_GROUPS)):
                step(BODIES, n)

        @block.scalar
        def _(act):
            def rows_out(r, n):
                act.wait_ge(conv_done, group_no(r, n))
                first = tiles_of(r, n)[0]
                for k0, count, rows in parts(r, n):
                    at = (k0 - first) * E
                    last = act.activation(h[0:rows, k0:k0 + count], conv_ps[n % 2][0:rows, at:at + count * E],
                                          ACT.Identity, scale=moments[0:rows, 5:6])
                last.then_inc(h_ready, 1)

            def turn_out(r, n):
                act.wait_ge(turned, group_no(r, n) + 1)
                first = tiles_of(r, n)[0]
                for k0, count, rows in parts(r, n):
                    at = (k0 - first) * P
                    last = act.copy(x_hat_t[:, k0:k0 + count, 0:rows],
                                    turn_ps[:, at:at + (count - 1) * P + rows])
                last.then_inc(x_hat_t_ready, 1)

            def values_out(r, k):
                rows = rows_of(r, k)
                act.wait_ge(vr_done, tile_no(r, k) + 1)
                act.copy(vr[0:rows, THIRD[k]], vr_ps[0:rows, 0:2 * E]).then_inc(vr_ready, 1)

            def state_out(r, k, half):
                act.wait_ge(state_done, token_no(r, k, half) + 1)
                act.copy(state[:, half], state_ps[:, 0:E]).then_inc(state_ready, 1)

            def step(r, n):
                tiles = tiles_of(r, n)
                after, evacuated = next_group(r, n, 1), next_group(r, n, NG - 1)
                for i, k in enumerate(tiles):
                    state_out(r, k, 0)
                    if k != tiles[-1]:
                        values_out(r, k + 1)
                    elif after:
                        turn_out(*after)
                    if rows_of(r, k) == P:
                        state_out(r, k, 1)
                        if after and k == tiles[-1]:
                            values_out(after[0], tiles_of(*after)[0])
                    if evacuated and i == 0:
                        act.wait_ge(h2_ready, tile_no(r, tiles[0]))
                        rows_out(*evacuated)

            act.dma_start(h[0:B, CLS], cls_tok.partition_broadcast(B)).then_inc(cls_in, 16)
            for tile, src in ((wq_sb, wq), (wk_sb, wk), (wv_sb, wv_t), (mem_sb, mem_t), (ident_sb, ident),
                              (same_sb, same_image)):
                act.dma_start(tile[:], src).then_inc(small_in, 16)
            act.wait_ge(bias_zero, 1)
            act.dma_start(bias_row[0:1, :], bias).then_inc(bias_in, 16)
            act.wait_ge(small_in, SMALLS)
            act.mul(w_vr[:, 0:E], wv_sb[:], LR).then_inc(w_vr_ready, 1)
            for blk in range(2):
                count = P if blk == 0 else PATCHES - P
                act.wait_ge(terms_done, blk + 1)
                act.copy(term_rows[0:count, blk],
                         out_ps[blk][0:count, 0:2 * E]).then_inc(term_rows_ready, 1)
            act.copy(ident_bf[:], ident_sb[:]).then_inc(ident_bf_ready, 1)
            act.wait_ge(product_done, 1)
            act.copy(w_vr[:, E:2 * E], vr_ps[:, 0:E]).then_inc(w_vr_ready, 1)
            act.wait_ge(turned, 1)
            act.copy(x_hat_t[:, CLS, 0:B], turn_ps[:, 0:B]).then_inc(x_hat_t_ready, 1)
            act.wait_ge(vr_done, 1)
            act.copy(vr[0:B, THIRD[CLS]], vr_ps[0:B, 0:2 * E]).then_inc(vr_ready, 1)
            act.wait_ge(state_done, 1)
            act.copy(state[:, 1], state_ps[:, 0:E]).then_inc(state_ready, 1)
            for n in range(2):
                act.wait_ge(conv_done, n + 1)
                k0, count = GROUPS[n][0], len(GROUPS[n])
                act.copy(result[:, k0:k0 + count], conv_ps[n][:, 0:count * E]).then_inc(raw_ready, 1)
            act.wait_ge(scales_done, 1)
            act.copy(scale_rows[:], out_ps[2][0:TERM_ROWS, 128:256]).then_inc(scale_rows_ready, 1)
            for n in range(2):
                act.wait_ge(first_terms_done, n + 1)
                k0, count = GROUPS[n][0], len(GROUPS[n])
                act.activation(h[:, k0:k0 + count], out_ps[2 * n][:, 0:count * E], ACT.Identity,
                               scale=moments[:, 5:6]).then_inc(first_terms_ready, 1)
            act.wait_ge(h_ready, 2)
            rows_out(0, 2)
            turn_out(0, 0)
            values_out(0, 0)
            with act.Fori(0, BODIES - 1) as r:
                for n in range(NG):
                    step(r, n)
            for n in range(NG):
                step(BODIES - 1, n)
            for n in range(len(TAIL_GROUPS)):
                step(BODIES, n)

        def scale_shift(eng, s, i, parity):
            if s == 0:
                windows = patch_rows[:, parity]
            else:
                slot, right = (i + (1 if s < 3 else 0)) & 3, (s - 1) % 2
                windows = offset_rows[:, slot, right:right + N]
            gains = gam[:, s, bass.ds(i * N, N)].unsqueeze(2).to_broadcast([P, N, B])
            return eng.tensor_tensor(scaled[:, s, parity * N:parity * N + N], windows, gains, ALU.mult)

        def scale_part(eng, shares, done, r, n, j, of):
            if n not in shares or (isinstance(r, int) and r > BODIES - 2):
                return
            parity = 1 if n == 0 else 0
            mine = shares[n]
            part = mine[len(mine) * j // of:len(mine) * (j + 1) // of]
            if not part:
                return
            if part[0] == mine[0] and n != 3:
                last_row = fixed(r, BODIES - 2) and not parity
                eng.wait_ge(patch_in[parity], 16 * (r + (3 - parity)))
                eng.wait_ge(offset_in[0], 64 * (r + 2))
                eng.wait_ge(offset_in[1], 64 * (r + (2 - parity)) - (32 if last_row else 0))
                if last_row:
                    eng.wait_ge(last_pad, 1)
                eng.wait_ge(conv_done, group_no(r, 3) if parity else group_no(r + 1, 1))
            for s in part:
                last = scale_shift(eng, s, 2 * r + (4 - parity), parity)
            if n != 2 and part[-1] == mine[-1]:
                last.then_inc(done, 1)

        def before(r, n):
            if fixed(r, 0) and n == 0:
                return -1, 3, [CLS], None
            r0, n0 = (r, n - 1) if n else (r - 1, NG - 1)
            if n0 == NG - 1:
                return r0, n0, tiles_of(r0, n0), (stored[n0], 32 * r0 + 16)
            return r0, n0, tiles_of(r0, n0), None if fixed(r0, 0) else (stored[n0], 32 * r0)

        @block.vector
        def _(dve):
            def ln1_stats_of(r, n):
                dve.wait_ge(h_ready, group_no(r, n))
                for k in tiles_of(r, n):
                    rows = rows_of(r, k)
                    last = dve.bn_stats(ln1_stats[0:rows, k], h[0:rows, k])
                return last

            def ln1_moments(r, n):
                for k in tiles_of(r, n):
                    rows = rows_of(r, k)
                    last = dve.bn_aggr(ln1_mv[0:rows, k], ln1_stats[0:rows, k])
                return last

            def ln1_add_eps(r, n):
                a, z = tiles_of(r, n)[0], tiles_of(r, n)[-1] + 1
                dve.tensor_scalar(ln1_var[:, a:z], ln1_mv[:, a:z, 1], LN_EPS, None, ALU.add).then_inc(ln1_var_ready, 1)

            def normalise(r, n):
                dve.wait_ge(ln1_rstd_ready, group_no(r, n) + 1)
                for k in tiles_of(r, n):
                    rows = rows_of(r, k)
                    last = dve.tensor_scalar(x_hat[0:rows, k], h[0:rows, k], ln1_mv[0:rows, k, 0:1],
                                             ln1_rstd[0:rows, k:k + 1], ALU.subtract, ALU.mult)
                last.then_inc(x_hat_ready, 1)

            def add_out(r, n, k):
                rows = rows_of(r, k)
                dve.wait_ge(out_done, tile_no(r, k) + 1)
                dve.tensor_tensor(h2[0:rows, k], out_ps[THIRD[k]][0:rows, 0:E], h[0:rows, k],
                                  ALU.add).then_inc(h2_ready, 1)
                dve.wait_ge(h2_ready, tile_no(r, k) + 1)
                last = dve.bn_stats(ln2_stats[0:rows, k], h2[0:rows, k])
                if fixed(r, BODIES) and k == HALF_TILE:
                    last.then_inc(last_stats_ready, 1)

            def ln2_moments(r, n, tiles, _):
                for k in tiles:
                    rows = B if fixed(r, -1) else rows_of(r, k)
                    last = dve.bn_aggr(ln2_mv[0:rows, k], ln2_stats[0:rows, k])
                return last

            def ln2_add_eps(r, n, tiles, _):
                a, z, rows = tiles[0], tiles[-1] + 1, B if fixed(r, -1) else P
                dve.tensor_scalar(ln2_var[0:rows, a:z], ln2_mv[0:rows, a:z, 1], LN_EPS, None,
                                  ALU.add).then_inc(ln2_var_ready, 1)

            def ln2_result(r, n, tiles, slots_free):
                group, rows = group_no(r, n), B if fixed(r, -1) else P
                a, z = tiles[0], tiles[-1] + 1
                dve.wait_ge(ln2_rstd_ready, group + 1)
                dve.tensor_scalar(ln2_gain[0:rows, a:z], ln2_rstd[0:rows, a:z], 1.0, None, ALU.add)
                dve.scalar_tensor_tensor(ln2_shift[0:rows, a:z], ln2_mv[0:rows, a:z, 0], -1.0,
                                         ln2_rstd[0:rows, a:z], ALU.mult, ALU.mult).then_inc(ln2_affine_ready, 1)
                dve.wait_ge(ln2_affine_ready, group + 1)
                if slots_free:
                    dve.wait_ge(*slots_free)
                for k in tiles:
                    m = min(rows, rows_of(r, k))
                    last = dve.tensor_scalar(result[0:m, k], h2[0:m, k], ln2_gain[0:m, k:k + 1],
                                             ln2_shift[0:m, k:k + 1], ALU.mult, ALU.add)
                last.then_inc(result_ready, 1)

            def step(r, n):
                tiles, prev = tiles_of(r, n), before(r, n)
                after, second = next_group(r, n, 1), next_group(r, n, 2)
                if after:
                    normalise(*after)
                if second:
                    ln1_stats_of(*second)
                scale_part(dve, VECTOR_SHIFTS, scaled_vector, r, n, 0, 3)
                add_out(r, n, tiles[0])
                if second:
                    ln1_moments(*second)
                ln2_moments(*prev).then_inc(mv_ready, 1)
                dve.wait_ge(mv_ready, group_no(r, n) + 3)
                if second:
                    ln1_add_eps(*second)
                ln2_add_eps(*prev)
                scale_part(dve, VECTOR_SHIFTS, scaled_vector, r, n, 1, 3)
                add_out(r, n, tiles[1])
                scale_part(dve, VECTOR_SHIFTS, scaled_vector, r, n, 2, 3)
                ln2_result(*prev)
                for k in tiles[2:]:
                    add_out(r, n, k)

            dve.memset(offset_rows[:, :, 0], 0.0)
            dve.memset(offset_rows[:, :, N], 0.0)
            dve.memset(offset_rows[0:B, 0, 1:N], 0.0).then_inc(pads_ready, 1)
            dve.memset(scale_cols[:], 0.0).then_inc(cols_zero, 1)
            dve.wait_ge(cls_in, 16)
            dve.bn_stats(ln1_stats[0:B, CLS], h[0:B, CLS]).then_inc(cls_stats_ready, 1)
            dve.wait_ge(cls_stats_ready, 1)
            dve.bn_aggr(ln1_mv[0:B, CLS], ln1_stats[0:B, CLS]).then_inc(mv_ready, 1)
            dve.wait_ge(mv_ready, 1)
            dve.tensor_scalar(ln1_var[0:B, CLS:CLS + 1], ln1_mv[0:B, CLS, 1:2], LN_EPS, None,
                              ALU.add).then_inc(ln1_var_ready, 1)
            dve.wait_ge(gamma_in, 16)
            dve.wait_ge(patch_in[0], 16)
            dve.wait_ge(first_offsets_in, 16 * 6)
            for s in range(3):
                last = scale_shift(dve, s, 0, 0)
            last.then_inc(scaled_vector, 1)
            dve.wait_ge(ln1_rstd_ready, 1)
            dve.tensor_scalar(x_hat[0:B, CLS], h[0:B, CLS], ln1_mv[0:B, CLS, 0:1],
                              ln1_rstd[0:B, CLS:CLS + 1], ALU.subtract, ALU.mult).then_inc(x_hat_ready, 1)
            dve.wait_ge(patch_in[1], 16)
            dve.wait_ge(offset_in[0], 64)
            for s in range(3):
                last = scale_shift(dve, s, 1, 1)
            last.then_inc(scaled_vector, 1)
            for i, (row, rows) in enumerate(STAT_CHUNKS):
                dve.wait_ge(images_in[i], 16)
                for j, (first, count, cols, _) in enumerate(STATS):
                    if row <= first + count - 1 < row + rows:
                        part = images[:, first:first + count]
                        if cols == "mid":
                            part = part[:, :, HALF:S - HALF]
                        else:
                            part = part.rearrange("p r (g q) -> p r g q", q=HALF)[:, :, 0:S // HALF:S // HALF - 1]
                        last_stats = dve.bn_stats(stats[:, 2 * j:2 * j + 2].rearrange("p a b -> p (a b)"), part)
            last_stats.then_inc(stats_step, 1)
            dve.wait_ge(stats_step, 1)
            dve.wait_ge(consts_ready, 1)
            dve.tensor_tensor(stat_tmp[:, 0], stats[:, :, 1], stat_w[:, 0], ALU.mult)
            dve.tensor_tensor(stat_tmp[:, 2], stats[:, :, 2], stat_w[:, 1], ALU.mult).then_inc(stats_step, 1)
            dve.wait_ge(stats_step, 2)
            dve.tensor_reduce(sums[:, 0:1], stat_tmp[:, 0], AX.X, ALU.add).then_inc(sums_ready, 1)
            dve.tensor_tensor(stat_tmp[:, 1], stat_tmp[:, 0], stats[:, :, 1], ALU.mult).then_inc(stats_step, 1)
            dve.wait_ge(stats_step, 3)
            dve.tensor_tensor(stat_tmp[:, 0], stat_tmp[:, 1], stat_tmp[:, 2], ALU.add).then_inc(stats_step, 1)
            dve.wait_ge(stats_step, 4)
            dve.tensor_reduce(sums[:, 1:2], stat_tmp[:, 0], AX.X, ALU.add).then_inc(sums_ready, 1)
            dve.wait_ge(image_sums_done, 1)
            dve.tensor_scalar(moments[:, 0:2], out_ps[2][:, 0:2], 1.0 / PIXELS, None, ALU.mult).then_inc(stats_step, 1)
            dve.wait_ge(stats_step, 5)
            dve.tensor_tensor(moments[:, 2:3], moments[:, 0:1], moments[:, 0:1], ALU.mult).then_inc(stats_step, 1)
            dve.wait_ge(stats_step, 6)
            dve.scalar_tensor_tensor(moments[:, 3:4], moments[:, 1:2], TOK_EPS, moments[:, 2:3], ALU.add,
                                     ALU.subtract).then_inc(image_var_ready, 1)
            dve.wait_ge(cols_zero, 1)
            for half in range(2):
                a = half * B
                dve.tensor_scalar(scale_cols[a:a + B, half, 1:2], moments[a:a + B, 0:1], -1.0, None,
                                  ALU.mult).then_inc(cols_ready, 1)
            dve.wait_ge(image_scale_ready, 1)
            for half in range(2):
                a = half * B
                dve.tensor_copy(scale_cols[a:a + B, half, 0:1], moments[a:a + B, 4:5]).then_inc(cols_ready, 1)
            def once_each(cols):
                return cols.unsqueeze(2).to_broadcast([P, 2, PARTS, 2])

            dve.wait_ge(cols_ready, 4)
            dve.tensor_copy(scale_parts[:, :, 0], once_each(scale_cols[:])).then_inc(scale_parts_ready, 1)
            dve.wait_ge(scale_parts_ready, 1)
            dve.tensor_tensor(scale_rest[:], scale_cols[:], scale_parts[:, :, 0, 0], ALU.subtract).then_inc(scale_rest_ready, 1)
            dve.wait_ge(scale_rest_ready, 1)
            dve.tensor_copy(scale_parts[:, :, 1], once_each(scale_rest[:])).then_inc(scale_parts_ready, 1)
            dve.wait_ge(scale_parts_ready, 2)
            dve.tensor_tensor(scale_parts[:, :, 2], once_each(scale_rest[:]), scale_parts[:, :, 1],
                              ALU.subtract).then_inc(scale_parts_ready, 1)
            dve.wait_ge(out_done, 1)
            dve.tensor_tensor(h2[0:B, CLS], out_ps[THIRD[CLS]][0:B, 0:E], h[0:B, CLS],
                              ALU.add).then_inc(h2_ready, 1)
            dve.wait_ge(h2_ready, 1)
            dve.bn_stats(ln2_stats[0:B, CLS], h2[0:B, CLS])
            dve.wait_ge(patch_in[0], 32)
            dve.wait_ge(conv_done, 2)
            for s in range(2):
                last = scale_shift(dve, s, 2, 0)
            last.then_inc(scaled_vector, 1)
            for n in range(2):
                k0, z = GROUPS[n][0], GROUPS[n][-1] + 1
                dve.wait_ge(first_terms_ready, n + 1)
                dve.scalar_tensor_tensor(h[:, k0:z], result[:, k0:z], moments[:, 5:6], h[:, k0:z], ALU.mult,
                                         ALU.add).then_inc(h_ready, 1)
                ln1_stats_of(0, n).then_inc(first_stats_ready, 1)
                dve.wait_ge(first_stats_ready, n + 1)
                ln1_moments(0, n).then_inc(mv_ready, 1)
                dve.wait_ge(mv_ready, n + 2)
                ln1_add_eps(0, n)
            normalise(0, 0)
            for n in range(NG):
                step(0, n)
            with dve.Fori(1, BODIES - 2) as r:
                for n in range(NG):
                    step(r, n)
            for r in (BODIES - 2, BODIES - 1):
                for n in range(NG):
                    step(r, n)
            for n in range(len(TAIL_GROUPS)):
                step(BODIES, n)
            prev = before(BODIES, len(TAIL_GROUPS))
            dve.wait_ge(last_stats_ready, 1)
            ln2_moments(*prev).then_inc(mv_ready, 1)
            dve.wait_ge(mv_ready, group_no(BODIES, len(TAIL_GROUPS)) + 3)
            ln2_add_eps(*prev)
            ln2_result(*prev)

        @block.gpsimd
        def _(pool):
            def ln1_power(r, n):
                a, z = tiles_of(r, n)[0], tiles_of(r, n)[-1] + 1
                pool.wait_ge(ln1_var_ready, group_no(r, n) + 1)
                pool.tensor_tensor(ln1_rstd[:, a:z], ln1_var[:, a:z], powers[:, 1:1 + z - a],
                                   ALU.pow).then_inc(ln1_rstd_ready, 1)

            def ln2_power(r, n, tiles, _):
                a, z, rows = tiles[0], tiles[-1] + 1, B if fixed(r, -1) else P
                pool.wait_ge(ln2_var_ready, group_no(r, n) + 1)
                pool.tensor_tensor(ln2_rstd[0:rows, a:z], ln2_var[0:rows, a:z], powers[0:rows, 1:1 + z - a],
                                   ALU.pow).then_inc(ln2_rstd_ready, 1)

            def step(r, n):
                second = next_group(r, n, 2)
                scale_part(pool, POOL_SHIFTS, scaled_pool, r, n, 0, 2)
                if second:
                    ln1_power(*second)
                ln2_power(*before(r, n))
                scale_part(pool, POOL_SHIFTS, scaled_pool, r, n, 1, 2)

            pool.memset(bias_row[:], 0.0).then_inc(bias_zero, 1)
            pool.memset(powers[:, 1:5], -0.5)
            pool.memset(powers[:, 0:1], 0.5)
            pool.memset(ones[:], 1.0)
            pool.memset(terms[:, PATCHES // 2], 0.0)
            for a, z in ((0, 2), (2, 4), (4, 6), (6, len(STATS))):
                _, rows, cols, w = STATS[a]
                count = rows * (S - 2 * HALF if cols == "mid" else 2 * HALF)
                pool.memset(stat_w[:, 0, 2 * a:2 * z], float(w * count // 2))
                last = pool.memset(stat_w[:, 1, 2 * a:2 * z], float(w))
            last.then_inc(consts_ready, 1)
            pool.wait_ge(consts_ready, 1)
            pool.wait_ge(ln1_var_ready, 1)
            pool.tensor_tensor(ln1_rstd[0:B, CLS:CLS + 1], ln1_var[0:B, CLS:CLS + 1], powers[0:B, 1:2],
                               ALU.pow).then_inc(ln1_rstd_ready, 1)
            pool.wait_ge(gamma_in, 16)
            pool.wait_ge(first_offsets_in, 16 * 6)
            for s in (3, 4):
                last = scale_shift(pool, s, 0, 0)
            last.then_inc(scaled_pool, 1)
            pool.wait_ge(offset_in[0], 64)
            for s in (3, 4):
                last = scale_shift(pool, s, 1, 1)
            last.then_inc(scaled_pool, 1)
            for blk in range(2):
                m = P if blk == 0 else PATCHES - P
                parts_of, rest = term_parts[0:m, blk], term_rest[0:m, blk]
                pool.wait_ge(term_rows_ready, blk + 1)
                pool.tensor_copy(parts_of[:, 0], term_rows[0:m, blk]).then_inc(term_step, 1)
                pool.wait_ge(term_step, 3 * blk + 1)
                pool.tensor_tensor(rest, term_rows[0:m, blk], parts_of[:, 0], ALU.subtract).then_inc(term_step, 1)
                pool.wait_ge(term_step, 3 * blk + 2)
                pool.tensor_copy(parts_of[:, 1], rest).then_inc(term_step, 1)
                pool.wait_ge(term_step, 3 * blk + 3)
                pool.tensor_tensor(parts_of[:, 2], rest, parts_of[:, 1], ALU.subtract).then_inc(term_parts_ready, 1)
            pool.wait_ge(conv_done, 2)
            pool.wait_ge(offset_in[1], 64)
            for s in (3, 4):
                scale_shift(pool, s, 2, 0)
            pool.wait_ge(image_var_ready, 1)
            pool.tensor_tensor(moments[:, 4:6], moments[:, 3:4].to_broadcast([P, 2]), powers[:, 0:2],
                               ALU.pow).then_inc(image_scale_ready, 1)
            scale_shift(pool, 2, 2, 0).then_inc(scaled_pool, 1)
            ln1_power(0, 0)
            ln1_power(0, 1)
            for n in range(NG):
                step(0, n)
            with pool.Fori(1, BODIES - 2) as r:
                for n in range(NG):
                    step(r, n)
            pool.wait_ge(scaled_vector, 2 * (BODIES - 1))
            pool.wait_ge(scaled_pool, 2 * (BODIES - 1) + 1)
            pool.wait_ge(ln2_rstd_ready, group_no(BODIES - 3, NG - 2) + 1)
            pool.memset(offset_rows[B:P, 1], 0.0).then_inc(last_pad, 1)
            pool.wait_ge(last_pad, 1)
            for r in (BODIES - 2, BODIES - 1):
                for n in range(NG):
                    step(r, n)
            for n in range(len(TAIL_GROUPS)):
                step(BODIES, n)
            ln2_power(*before(BODIES, len(TAIL_GROUPS)))


def kernel(x, cls_tok, L0_tok_gamma, L0_tok_beta, L0_tok_W, L0_tok_b, L0_attn_Wq, L0_attn_Wk, L0_attn_Wv,
           L0_attn_memory0, L0_ffn_W, L0_ffn_b):
    import numpy as np
    import concourse.bacc as bacc
    from concourse.bass_utils import run_bass_kernel_spmd

    def windows(a):
        m = a.shape[0]
        a = a.reshape(m, 2, N, 2, HALF, N, 2, HALF)
        return a.transpose(3, 6, 1, 4, 7, 0, 2, 5).reshape(P, m, N, N)

    x, gamma, beta, w = (np.asarray(a) for a in (x, L0_tok_gamma, L0_tok_beta, L0_tok_W))
    arrays = {
        "x_rows": x.reshape(P, S, S),
        "x_win": windows(x).transpose(0, 2, 3, 1),
        "gamma": windows(gamma.reshape(SHIFTS, 2, S, S)).reshape(P, SHIFTS, PATCHES),
        "beta": windows(beta.reshape(SHIFTS, 2, S, S)).reshape(P, SHIFTS, PATCHES),
        "weight": w.reshape(E, SHIFTS, 2, 2, HALF, 2, HALF).transpose(3, 5, 2, 4, 6, 1, 0).reshape(P, SHIFTS, E),
        "bias": np.asarray(L0_tok_b).reshape(1, E),
        "cls_tok": np.asarray(cls_tok).reshape(E),
        "wq": np.asarray(L0_attn_Wq),
        "wk": np.asarray(L0_attn_Wk),
        "wv_t": np.asarray(L0_attn_Wv).T,
        "mem_t": np.asarray(L0_attn_memory0).T,
        "ident": np.eye(P, dtype=np.float32),
        "same_image": np.kron(np.eye(B, dtype=np.float32), np.ones((2, 1), np.float32))[:, list(range(B)) * 2],
    }
    nc = bacc.Bacc("TRN2", target_bir_lowering=False, num_devices=1)
    in_map, args = {}, []
    for name, a in arrays.items():
        in_map[name] = np.ascontiguousarray(a)
        args.append(nc.dram_tensor(name, in_map[name].shape, F32, kind="ExternalInput").ap())
    args.append(nc.dram_tensor("out", (B, PATCHES + 1, E), F32, kind="ExternalOutput").ap())
    args.append(nc.dram_tensor("parked", (2 * PARTS, PATCHES, E), BF16, kind="Internal").ap())
    tower(nc, *args)
    return run_bass_kernel_spmd(nc, [in_map], core_ids=[0]).results[0]["out"]
```

```python
from contextlib import ExitStack

import concourse.bass as bass
from concourse import mybir

F32 = mybir.dt.float32
BF16 = mybir.dt.bfloat16
F32R = mybir.dt.float32r
ALU = mybir.AluOpType
ACT = mybir.ActivationFunctionType
AX = mybir.AxisListType

P = 128
B = 64
E = 128
S = 104
HALF = 4
N = S // (2 * HALF)
PATCHES = N * N
SHIFTS = 5
LR = 0.01
LN_EPS = 1e-5
TOK_EPS = 1e-7
PIXELS = 2 * SHIFTS * S * S

TILES = N
TOKENS = 2 * N
BODIES = N // 2
GROUPS = [range(0, 4), range(4, 7), range(7, 10), range(10, 13)]
TAIL_GROUPS = [range(0, 4), range(4, 7)]
NG = len(GROUPS)
HALF_TILE = N // 2
CLS = TILES - 1
THIRD = [0, 1, 2, 0, 1, 2, 0, 1, 2, 0, 1, 2, 1]

STAT_CHUNKS = [(0, 28), (28, 24), (52, 12), (64, 16), (80, 12), (92, 12)]
STATS = [(0, 4, "mid", 3), (100, 4, "mid", 3), (0, 4, "edge", 2), (100, 4, "edge", 2),
         (4, 48, "edge", 3), (52, 48, "edge", 3)] + [(4 * q, 4, "mid", 5) for q in range(1, 25)]

VECTOR_SHIFTS = {0: [[0], [1], [2]], 2: [[0], [1], []], 3: [[2], [], []]}
POOL_SHIFTS = {0: [[3], [4]], 2: [[3], []], 3: [[4], []]}
PARTS = 3
TERM_ROWS = PARTS * PARTS * 4
SMALLS = 16 * 6


def fixed(r, value):
    return isinstance(r, int) and r == value


def tower(nc, x_rows, x_win, gamma, beta, weight, bias, cls_tok, wq, wk, wv_t, mem_t, ident, same_image, out, parked):
    with ExitStack() as ctx:
        def sb(name, shape, dtype=F32):
            return ctx.enter_context(nc.sbuf_tensor(name, shape, dtype))

        def pb(name):
            return ctx.enter_context(nc.psum_tensor(name, [P, 512], F32))

        def sem(name):
            return ctx.enter_context(nc.semaphore(name))

        images = sb("images", [P, S, S])
        patch_rows = sb("patch_rows", [P, 2, N, B])
        offset_rows = sb("offset_rows", [P, 4, N + 1, B])
        gam = sb("gam", [P, SHIFTS, PATCHES])
        bet = sb("bet", [P, SHIFTS, PATCHES])
        wt = sb("wt", [P, SHIFTS, E])
        scaled = sb("scaled", [P, SHIFTS, TOKENS, B])
        terms = sb("terms", [TERM_ROWS, PATCHES // 2 + 1, E], BF16)
        term_rows = sb("term_rows", [P, 2, 2, E])
        term_rest = sb("term_rest", [P, 2, 2, E])
        term_parts = sb("term_parts", [P, 2, PARTS, 2, E], BF16)
        scale_rows = sb("scale_rows", [TERM_ROWS, P], BF16)
        scale_cols = sb("scale_cols", [P, 2, 2])
        scale_rest = sb("scale_rest", [P, 2, 2])
        scale_parts = sb("scale_parts", [P, 2, PARTS, PARTS, 2], BF16)
        ident_bf = sb("ident_bf", [P, P], BF16)
        bias_row = sb("bias_row", [P, E])
        ones = sb("ones", [P, P])
        wq_sb = sb("wq_sb", [P, E])
        wk_sb = sb("wk_sb", [P, E])
        wv_sb = sb("wv_sb", [P, E])
        mem_sb = sb("mem_sb", [P, E])
        ident_sb = sb("ident_sb", [P, P])
        same_sb = sb("same_sb", [P, P])
        w_vr = sb("w_vr", [P, 2 * E])
        stats = sb("stats", [P, 2 * len(STATS), 3])
        stat_w = sb("stat_w", [P, 2, 2 * len(STATS)])
        stat_tmp = sb("stat_tmp", [P, 3, 2 * len(STATS)])
        sums = sb("sums", [P, 2])
        moments = sb("moments", [P, 6])
        powers = sb("powers", [P, 5])
        h = sb("h", [P, TILES, E])
        x_hat = sb("x_hat", [P, TILES, E])
        x_hat_t = sb("x_hat_t", [P, TILES, P])
        x_parts = sb("x_parts", [P, 2, TILES, P], F32R)
        w_parts = sb("w_parts", [P, 2, 2 * E], F32R)
        vr = sb("vr", [P, 3, 2 * E])
        state = sb("state", [P, 3, 2, E])
        h2 = sb("h2", [P, TILES, E])
        result = sb("result", [P, TILES, E])
        ln1_stats = sb("ln1_stats", [P, TILES, 6])
        ln1_mv = sb("ln1_mv", [P, TILES, 2])
        ln1_var = sb("ln1_var", [P, TILES])
        ln1_rstd = sb("ln1_rstd", [P, TILES])
        ln2_stats = sb("ln2_stats", [P, TILES, 6])
        ln2_mv = sb("ln2_mv", [P, TILES, 2])
        ln2_var = sb("ln2_var", [P, TILES])
        ln2_rstd = sb("ln2_rstd", [P, TILES])
        ln2_gain = sb("ln2_gain", [P, TILES])
        ln2_shift = sb("ln2_shift", [P, TILES])

        conv_ps = [pb("conv0"), pb("conv1")]
        turn_ps = pb("turn")
        vr_ps = pb("vr_ps")
        state_ps = pb("state_ps")
        out_ps = [pb("out0"), pb("out1"), pb("out2")]

        images_in = [sem(f"images_in{i}") for i in range(len(STAT_CHUNKS))]
        patch_in = [sem("patch_in_even"), sem("patch_in_odd")]
        first_offsets_in = sem("first_offsets_in")
        offset_in = [sem("offset_in_even"), sem("offset_in_odd")]
        gamma_in = sem("gamma_in")
        tables_in = sem("tables_in")
        small_in = sem("small_in")
        cls_in = sem("cls_in")
        bias_in = sem("bias_in")
        terms_parked = sem("terms_parked")
        terms_in = sem("terms_in")
        stored = [sem(f"stored{i}") for i in range(NG)]
        pads_ready = sem("pads_ready")
        bias_zero = sem("bias_zero")
        cols_zero = sem("cols_zero")
        consts_ready = sem("consts_ready")
        terms_done = sem("terms_done")
        term_rows_ready = sem("term_rows_ready")
        term_step = sem("term_step")
        term_parts_ready = sem("term_parts_ready")
        ident_bf_ready = sem("ident_bf_ready")
        product_done = sem("product_done")
        w_vr_ready = sem("w_vr_ready")
        stats_step = sem("stats_step")
        sums_ready = sem("sums_ready")
        image_sums_done = sem("image_sums_done")
        image_var_ready = sem("image_var_ready")
        image_scale_ready = sem("image_scale_ready")
        cols_ready = sem("cols_ready")
        scales_done = sem("scales_done")
        scale_rest_ready = sem("scale_rest_ready")
        scale_parts_ready = sem("scale_parts_ready")
        scale_rows_ready = sem("scale_rows_ready")
        scaled_vector = sem("scaled_vector")
        scaled_pool = sem("scaled_pool")
        last_pad = sem("last_pad")
        conv_done = sem("conv_done")
        raw_ready = sem("raw_ready")
        first_terms_done = sem("first_terms_done")
        first_h_ready = sem("first_h_ready")
        h_ready = sem("h_ready")
        cls_stats_ready = sem("cls_stats_ready")
        mv_ready = sem("mv_ready")
        ln1_var_ready = sem("ln1_var_ready")
        ln1_rstd_ready = sem("ln1_rstd_ready")
        x_hat_ready = sem("x_hat_ready")
        turned = sem("turned")
        x_hat_t_ready = sem("x_hat_t_ready")
        x_parts_ready = sem("x_parts_ready")
        w_high_ready = sem("w_high_ready")
        w_parts_ready = sem("w_parts_ready")
        vr_done = sem("vr_done")
        vr_ready = sem("vr_ready")
        state_done = sem("state_done")
        state_ready = sem("state_ready")
        out_done = sem("out_done")
        h2_ready = sem("h2_ready")
        first_stats_ready = sem("first_stats_ready")
        last_stats_ready = sem("last_stats_ready")
        ln2_var_ready = sem("ln2_var_ready")
        ln2_rstd_ready = sem("ln2_rstd_ready")
        ln2_affine_ready = sem("ln2_affine_ready")
        result_ready = sem("result_ready")

        def group_no(r, n):
            return NG * r + (n + 1)

        def tile_no(r, k):
            return TILES * r + (k + 1)

        def token_no(r, k, half):
            return TOKENS * r + (2 * k + half + 1)

        def tiles_of(r, n):
            return (TAIL_GROUPS if fixed(r, BODIES) else GROUPS)[n]

        def rows_of(r, k):
            return B if fixed(r, BODIES) and k == HALF_TILE else P

        def parts(r, n):
            tiles = tiles_of(r, n)
            if rows_of(r, tiles[-1]) == B:
                return [(tiles[0], len(tiles) - 1, P), (tiles[-1], 1, B)]
            return [(tiles[0], len(tiles), P)]

        def scaled_rows(r, k):
            return 2 * r + (1 if 2 * k + 1 < N or rows_of(r, k) == B else 2)

        def next_group(r, n, ahead):
            n += ahead
            if n >= NG and not fixed(r, BODIES):
                r, n = r + 1, n - NG
            return None if fixed(r, BODIES) and n >= len(TAIL_GROUPS) else (r, n)

        def in_parts(r, n):
            return not (fixed(r, BODIES) or (fixed(r, BODIES - 1) and n == NG - 1) or (fixed(r, 0) and n == 0))

        def tile_after_next(r, n, i):
            tiles = tiles_of(r, n)
            if i + 2 < len(tiles):
                return r, n, tiles[i + 2]
            after = next_group(r, n, 1)
            return (*after, tiles_of(*after)[i + 2 - len(tiles)]) if after else None

        block = ctx.enter_context(nc.Block())

        @block.sync
        def _(sp):
            def load_patch_row(i, slot):
                sp.dma_start(patch_rows[:, slot], x_win[:, i]).then_inc(patch_in[slot], 16)

            def load_offset_row(i, slot, landed, upper=True, lower=True):
                for a in range(2):
                    if (upper, lower)[a]:
                        for b in range(2):
                            q, src = 32 * (2 * a + b), 32 * (2 * (1 - a) + (1 - b))
                            sp.dma_start(offset_rows[q:q + 32, slot, 1 - b:1 - b + N],
                                         x_win[src:src + 32, i - 1 + a]).then_inc(landed, 16)

            def store(r, n):
                tiles = tiles_of(r, n)
                for half in range(2):
                    k0, count = tiles[0], len(tiles) - (half if rows_of(r, tiles[-1]) == B else 0)
                    sp.dma_start(out[:, bass.ds(token_no(r, k0, half), count, 2)],
                                 result[half * B:half * B + B, k0:k0 + count]).then_inc(stored[n], 16)

            sp.dma_start(gam[:], gamma).then_inc(gamma_in, 16)
            sp.dma_start(wt[:], weight).then_inc(tables_in, 16)
            sp.dma_start(bet[:], beta).then_inc(tables_in, 16)
            load_patch_row(0, 0)
            sp.wait_ge(pads_ready, 1)
            load_offset_row(0, 0, first_offsets_in, upper=False)
            load_offset_row(1, 1, first_offsets_in)
            for i, (row, rows) in enumerate(STAT_CHUNKS):
                sp.dma_start(images[:, row:row + rows], x_rows[:, row:row + rows]).then_inc(images_in[i], 16)
                if i == 1:
                    load_offset_row(2, 2, offset_in[0])
                    load_patch_row(1, 1)

            for blk in range(2):
                sp.wait_ge(term_parts_ready, blk + 1)
                count = P if blk == 0 else PATCHES - P
                for half in range(2):
                    m = (count + 1 - half) // 2
                    rows_of_tiles = parked[half, :, blk * B:blk * B + m].rearrange("k m e -> m k e")
                    patches = term_parts[half:count:2, blk].rearrange("p a k e -> p (a k) e")
                    sp.dma_start(rows_of_tiles, patches).then_inc(terms_parked, 16)
            load_offset_row(3, 3, offset_in[1])
            sp.wait_ge(scaled_vector, 1)
            sp.wait_ge(scaled_pool, 1)
            load_patch_row(2, 0)
            sp.wait_ge(consts_ready, 1)
            sp.wait_ge(terms_parked, 64)
            for i in range(2 * PARTS):
                half, row = i // PARTS, 2 * PARTS * i
                m = (PATCHES + 1 - half) // 2
                sp.dma_start(terms[row:row + 2 * PARTS, 0:m], parked[half, :, 0:m]).then_inc(terms_in, 16)
            sp.wait_ge(scaled_vector, 2)
            sp.wait_ge(scaled_pool, 2)
            sp.wait_ge(offset_in[0], 64)
            load_patch_row(3, 1)
            load_offset_row(4, 0, offset_in[0])
            sp.wait_ge(offset_in[1], 64)
            load_offset_row(5, 1, offset_in[1])
            sp.wait_ge(scaled_vector, 3)
            sp.wait_ge(scaled_pool, 3)
            load_patch_row(4, 0)

            def body(r, loads=True, lower=True):
                if fixed(r, 0):
                    sp.wait_ge(result_ready, 1)
                    sp.dma_start(out[:, 0], result[0:B, CLS]).then_inc(stored[NG - 1], 16)
                else:
                    sp.wait_ge(result_ready, group_no(r - 1, NG - 1) + 1)
                    store(r - 1, NG - 1)
                if loads:
                    for half in range(2):
                        sp.wait_ge(offset_in[half], 64 * (r + 2))
                    sp.wait_ge(scaled_vector, 2 * r + 4)
                    sp.wait_ge(scaled_pool, 2 * r + 4)
                    load_patch_row(2 * r + 5, 1)
                    for half in range(2):
                        load_offset_row(2 * r + (6 + half), 2 * ((r + 1) & 1) + half, offset_in[half],
                                        lower=lower or half == 0)
                for n in range(NG - 1):
                    sp.wait_ge(result_ready, group_no(r, n) + 1)
                    store(r, n)
                if loads:
                    sp.wait_ge(scaled_vector, 2 * r + 5)
                    sp.wait_ge(scaled_pool, 2 * r + 5)
                    load_patch_row(2 * r + 6, 0)

            body(0)
            with sp.Fori(1, BODIES - 3) as r:
                body(r)
            body(BODIES - 3, lower=False)
            body(BODIES - 2, loads=False)
            body(BODIES - 1, loads=False)
            for r, n in ((BODIES - 1, NG - 1), (BODIES, 0), (BODIES, 1)):
                sp.wait_ge(result_ready, group_no(r, n) + 1)
                store(r, n)
            for n in range(NG):
                sp.wait_ge(stored[n], 32 * BODIES + (32, 32, 0, 16)[n])

        @block.tensor
        def _(pe):
            def conv(r, n, a, b):
                tiles, ps = tiles_of(r, n), conv_ps[n % 2]
                for i in range(a, min(b, SHIFTS * len(tiles))):
                    k, s = tiles[i // SHIFTS], i % SHIFTS
                    at, rows = (k - tiles[0]) * E, rows_of(r, k)
                    if s == 0:
                        pe.wait_ge(scaled_vector, scaled_rows(r, k))
                        pe.wait_ge(scaled_pool, scaled_rows(r, k))
                    pe.matmul(ps[0:rows, at:at + E], scaled[:, s, 2 * k:2 * k + rows // B], wt[:, s],
                              start=(i == 0), stop=False, skip_group_check=True)
                if b > SHIFTS * len(tiles):
                    for k0, count, rows in parts(r, n):
                        at = (k0 - tiles[0]) * E
                        last = pe.matmul(ps[0:rows, at:at + count * E], scale_rows[:, 0:rows],
                                         terms[:, bass.ds(TILES * r + k0, count)],
                                         start=False, stop=True, skip_group_check=True)
                    last.then_inc(conv_done, 1)

            def conv_early(n):
                tiles = GROUPS[n]
                for k in tiles:
                    pe.wait_ge(scaled_vector, scaled_rows(0, k))
                    pe.wait_ge(scaled_pool, scaled_rows(0, k))
                    for s in range(SHIFTS):
                        last = pe.matmul(conv_ps[n][:, (k - tiles[0]) * E:(k - tiles[0]) * E + E],
                                         scaled[:, s, 2 * k:2 * k + 2], wt[:, s], start=(k == tiles[0] and s == 0),
                                         stop=(s == SHIFTS - 1), skip_group_check=True)
                last.then_inc(conv_done, 1)

            def turn(r, n):
                pe.wait_ge(x_hat_ready, group_no(r, n) + 1)
                pe.wait_ge(x_hat_t_ready, group_no(r, n))
                tiles = tiles_of(r, n)
                for k in tiles:
                    at, rows = (k - tiles[0]) * P, rows_of(r, k)
                    last = pe.transpose(turn_ps[:, at:at + rows], x_hat[0:rows, k], ident_sb[0:rows, 0:rows])
                last.then_inc(turned, 1)

            def values(r, n, k):
                pe.wait_ge(vr_ready, tile_no(r, k))
                rows = rows_of(r, k)
                if not in_parts(r, n):
                    pe.wait_ge(x_hat_t_ready, group_no(r, n) + 1)
                    pe.matmul(vr_ps[0:rows, 0:2 * E], x_hat_t[:, k, 0:rows], w_vr[:], start=True,
                              stop=True).then_inc(vr_done, 1)
                    return
                pe.wait_ge(x_parts_ready, group_no(r, n) - 1)
                for i, (x_part, w_part) in enumerate(((1, 0), (0, 1), (0, 0))):
                    last = pe.matmul(vr_ps[0:rows, 0:2 * E], x_parts[:, x_part, k, 0:rows], w_parts[:, w_part],
                                     start=(i == 0), stop=(i == 2))
                last.then_inc(vr_done, 1)

            def update(r, k, half):
                base = half * B
                pe.wait_ge(vr_ready, tile_no(r, k) + 1)
                pe.wait_ge(state_ready, token_no(r, k, half))
                pe.matmul(state_ps[:, 0:E], vr[base:base + B, THIRD[k], E:2 * E],
                          vr[base:base + B, THIRD[k], 0:E], start=False, stop=False,
                          skip_group_check=True).then_inc(state_done, 1)

            def read(r, k, half):
                base = half * B
                pe.wait_ge(state_ready, token_no(r, k, half) + 1)
                if half == 0 and k > 0:
                    pe.wait_ge(h2_ready, tile_no(r, k) - 1)
                last = pe.matmul(out_ps[THIRD[k]][base:base + B, 0:E], x_hat_t[:, k, base:base + B],
                                 state[:, THIRD[k], half], start=True, stop=True)
                if half == 1 or rows_of(r, k) == B:
                    last.then_inc(out_done, 1)

            def read_tile(r, k):
                read(r, k, 0)
                if rows_of(r, k) == P:
                    read(r, k, 1)

            def step(r, n, early=0):
                tiles = tiles_of(r, n)
                ahead, after = next_group(r, n, NG), next_group(r, n, 1)
                total = SHIFTS * len(tiles_of(*ahead)) + 1 - early if ahead else 0

                def conv_share(j):
                    if ahead:
                        if j == 0:
                            pe.wait_ge(h_ready, group_no(*ahead) - 2)
                        conv(*ahead, early + total * j // (2 * len(tiles)), early + total * (j + 1) // (2 * len(tiles)))

                for i, k in enumerate(tiles):
                    update(r, k, 0)
                    if k > 0:
                        read_tile(r, k - 1)
                    elif not fixed(r, 0):
                        read_tile(r - 1, TILES - 1)
                    if after and i == 0:
                        turn(*after)
                    conv_share(2 * i)
                    if rows_of(r, k) == P:
                        update(r, k, 1)
                    second = tile_after_next(r, n, i)
                    if second:
                        values(*second)
                    if rows_of(r, k) == P:
                        conv_share(2 * i + 1)

            pe.wait_ge(gamma_in, 16)
            pe.wait_ge(tables_in, 32)
            pe.wait_ge(consts_ready, 1)
            pe.wait_ge(bias_in, 16)
            for blk in range(2):
                count = P if blk == 0 else PATCHES - P
                for kind, table in enumerate((bet, gam)):
                    for s in range(SHIFTS):
                        last = pe.matmul(out_ps[blk][0:count, kind * E:kind * E + E],
                                         table[:, s, blk * P:blk * P + count], wt[:, s],
                                         start=(s == 0), stop=(kind == 1 and s == SHIFTS - 1))
                    if kind == 0:
                        last = pe.matmul(out_ps[blk][0:count, 0:E], ones[:, 0:count], bias_row[:],
                                         start=False, stop=True)
                last.then_inc(terms_done, 1)
            pe.wait_ge(small_in, SMALLS)
            pe.matmul(vr_ps[:, 0:E], wk_sb[:], wq_sb[:], start=True, stop=True).then_inc(product_done, 1)
            pe.matmul(state_ps[:, 0:E], wq_sb[:], mem_sb[:], start=True, stop=False, skip_group_check=True)
            pe.wait_ge(x_hat_ready, 1)
            pe.transpose(turn_ps[:, 0:B], x_hat[0:B, CLS], ident_sb[0:B, 0:B]).then_inc(turned, 1)
            pe.wait_ge(x_hat_t_ready, 1)
            pe.wait_ge(w_vr_ready, 2)
            pe.matmul(vr_ps[0:B, 0:2 * E], x_hat_t[:, CLS, 0:B], w_vr[:], start=True,
                      stop=True).then_inc(vr_done, 1)
            conv_early(0)
            pe.wait_ge(vr_ready, 1)
            pe.matmul(state_ps[:, 0:E], vr[0:B, THIRD[CLS], E:2 * E], vr[0:B, THIRD[CLS], 0:E], start=False,
                      stop=False, skip_group_check=True).then_inc(state_done, 1)
            pe.wait_ge(state_ready, 1)
            pe.wait_ge(term_rows_ready, 2)
            pe.matmul(out_ps[THIRD[CLS]][0:B, 0:E], x_hat_t[:, CLS, 0:B], state[:, THIRD[CLS], 1], start=True,
                      stop=True).then_inc(out_done, 1)
            conv_early(1)
            pe.wait_ge(raw_ready, 1)
            conv(0, 2, 0, SHIFTS * len(GROUPS[2]))
            pe.wait_ge(sums_ready, 2)
            pe.matmul(out_ps[2][:, 0:2], same_sb[:], sums[:], start=True, stop=True).then_inc(image_sums_done, 1)
            pe.wait_ge(raw_ready, 2)
            meanwhile = SHIFTS * len(GROUPS[3]) - 4
            conv(0, 3, 0, meanwhile)
            pe.wait_ge(scale_parts_ready, 3)
            pe.wait_ge(ident_bf_ready, 1)
            pe.matmul(out_ps[2][0:TERM_ROWS, 128:256], scale_parts[:].rearrange("p h a b k -> p (h a b k)"),
                      ident_bf[:], start=True, stop=True).then_inc(scales_done, 1)
            conv(0, 3, meanwhile, SHIFTS * len(GROUPS[3]))
            pe.wait_ge(scale_rows_ready, 1)
            pe.wait_ge(terms_in, 16 * 2 * PARTS)
            for n in range(2):
                k0, count = GROUPS[n][0], len(GROUPS[n])
                pe.matmul(out_ps[2 * n][:, 0:count * E], scale_rows[:], terms[:, k0:k0 + count], start=True,
                          stop=True).then_inc(first_terms_done, 1)
            for n in range(2, NG):
                conv(0, n, SHIFTS * len(GROUPS[n]), SHIFTS * len(GROUPS[n]) + 1)
            pe.wait_ge(h_ready, 2)
            pe.wait_ge(h_ready, 3)
            conv(1, 0, 0, 10)
            turn(0, 0)
            pe.wait_ge(w_parts_ready, 1)
            conv(1, 0, 10, 14)
            values(0, 0, 0)
            conv(1, 0, 14, 16)
            values(0, 0, 1)
            step(0, 0, early=16)
            for n in range(1, NG):
                step(0, n)
            with pe.Fori(1, BODIES - 1) as r:
                for n in range(NG):
                    step(r, n)
            for n in range(NG):
                step(BODIES - 1, n)
            for n in range(len(TAIL_GROUPS)):
                step(BODIES, n)
            read_tile(BODIES, HALF_TILE)

        @block.scalar
        def _(act):
            def rows_out(r, n):
                act.wait_ge(conv_done, group_no(r, n))
                first = tiles_of(r, n)[0]
                for k0, count, rows in parts(r, n):
                    at = (k0 - first) * E
                    last = act.activation(h[0:rows, k0:k0 + count], conv_ps[n % 2][0:rows, at:at + count * E],
                                          ACT.Identity, scale=moments[0:rows, 5:6])
                last.then_inc(h_ready, 1)

            def turn_out(r, n, high):
                act.wait_ge(turned, group_no(r, n) + 1)
                first = tiles_of(r, n)[0]
                for k0, count, rows in parts(r, n):
                    at = (k0 - first) * P
                    dst = x_parts[:, 0] if high else x_hat_t
                    last = act.copy(dst[:, k0:k0 + count, 0:rows], turn_ps[:, at:at + (count - 1) * P + rows])
                if not high:
                    last.then_inc(x_hat_t_ready, 1)

            def values_out(r, k):
                rows = rows_of(r, k)
                act.wait_ge(vr_done, tile_no(r, k) + 1)
                act.copy(vr[0:rows, THIRD[k]], vr_ps[0:rows, 0:2 * E]).then_inc(vr_ready, 1)

            def state_out(r, k, half):
                act.wait_ge(state_done, token_no(r, k, half) + 1)
                act.copy(state[:, THIRD[k], half], state_ps[:, 0:E]).then_inc(state_ready, 1)

            def step(r, n):
                tiles = tiles_of(r, n)
                after, evacuated = next_group(r, n, 1), next_group(r, n, NG - 1)
                for i, k in enumerate(tiles):
                    state_out(r, k, 0)
                    if after and i == 0 and in_parts(*after):
                        turn_out(*after, True)
                    if rows_of(r, k) == P:
                        state_out(r, k, 1)
                    if after and i == 0:
                        turn_out(*after, False)
                    second = tile_after_next(r, n, i)
                    if second:
                        values_out(second[0], second[2])
                    if evacuated and i == 0:
                        act.wait_ge(h2_ready, tile_no(r, tiles[0]))
                        rows_out(*evacuated)

            act.dma_start(h[0:B, CLS], cls_tok.partition_broadcast(B)).then_inc(cls_in, 16)
            for tile, src in ((wq_sb, wq), (wk_sb, wk), (wv_sb, wv_t), (mem_sb, mem_t), (ident_sb, ident),
                              (same_sb, same_image)):
                act.dma_start(tile[:], src).then_inc(small_in, 16)
            act.wait_ge(bias_zero, 1)
            act.dma_start(bias_row[0:1, :], bias).then_inc(bias_in, 16)
            act.wait_ge(small_in, SMALLS)
            act.mul(w_vr[:, 0:E], wv_sb[:], LR).then_inc(w_vr_ready, 1)
            for blk in range(2):
                count = P if blk == 0 else PATCHES - P
                act.wait_ge(terms_done, blk + 1)
                act.copy(term_rows[0:count, blk],
                         out_ps[blk][0:count, 0:2 * E]).then_inc(term_rows_ready, 1)
            act.copy(ident_bf[:], ident_sb[:]).then_inc(ident_bf_ready, 1)
            act.wait_ge(product_done, 1)
            act.copy(w_vr[:, E:2 * E], vr_ps[:, 0:E]).then_inc(w_vr_ready, 1)
            act.wait_ge(turned, 1)
            act.copy(x_hat_t[:, CLS, 0:B], turn_ps[:, 0:B]).then_inc(x_hat_t_ready, 1)
            act.wait_ge(vr_done, 1)
            act.copy(vr[0:B, THIRD[CLS]], vr_ps[0:B, 0:2 * E]).then_inc(vr_ready, 1)
            act.wait_ge(state_done, 1)
            act.copy(state[:, THIRD[CLS], 1], state_ps[:, 0:E]).then_inc(state_ready, 1)
            for n in range(2):
                act.wait_ge(conv_done, n + 1)
                k0, count = GROUPS[n][0], len(GROUPS[n])
                act.copy(result[:, k0:k0 + count], conv_ps[n][:, 0:count * E]).then_inc(raw_ready, 1)
            act.wait_ge(scales_done, 1)
            act.copy(scale_rows[:], out_ps[2][0:TERM_ROWS, 128:256]).then_inc(scale_rows_ready, 1)
            for n in range(2):
                act.wait_ge(first_terms_done, n + 1)
                k0, count = GROUPS[n][0], len(GROUPS[n])
                act.activation(h[:, k0:k0 + count], out_ps[2 * n][:, 0:count * E], ACT.Identity,
                               scale=moments[:, 5:6]).then_inc(h_ready, 1)
            rows_out(0, 2)
            turn_out(0, 0, False)
            values_out(0, 0)
            values_out(0, 1)
            with act.Fori(0, BODIES - 1) as r:
                for n in range(NG):
                    step(r, n)
            for n in range(NG):
                step(BODIES - 1, n)
            for n in range(len(TAIL_GROUPS)):
                step(BODIES, n)

        def scale_shift(eng, s, i, parity):
            if s == 0:
                windows = patch_rows[:, parity]
            else:
                slot, right = (i + (1 if s < 3 else 0)) & 3, (s - 1) % 2
                windows = offset_rows[:, slot, right:right + N]
            gains = gam[:, s, bass.ds(i * N, N)].unsqueeze(2).to_broadcast([P, N, B])
            return eng.tensor_tensor(scaled[:, s, parity * N:parity * N + N], windows, gains, ALU.mult)

        def scale_part(eng, shares, done, r, n, j):
            if n not in shares or (isinstance(r, int) and r > BODIES - 2):
                return
            parity = 1 if n == 0 else 0
            part = shares[n][j]
            if not part:
                return
            if j == 0 and n != 3:
                last_row = fixed(r, BODIES - 2) and not parity
                eng.wait_ge(patch_in[parity], 16 * (r + (3 - parity)))
                eng.wait_ge(offset_in[0], 64 * (r + 2))
                eng.wait_ge(offset_in[1], 64 * (r + (2 - parity)) - (32 if last_row else 0))
                if last_row:
                    eng.wait_ge(last_pad, 1)
                eng.wait_ge(conv_done, group_no(r, 3) if parity else group_no(r + 1, 1))
            for s in part:
                last = scale_shift(eng, s, 2 * r + (4 - parity), parity)
            if n != 2 and part == [p for p in shares[n] if p][-1]:
                last.then_inc(done, 1)

        def before(r, n):
            if fixed(r, 0) and n == 0:
                return -1, NG - 1, [CLS], None
            r0, n0 = (r, n - 1) if n else (r - 1, NG - 1)
            if n0 == NG - 1:
                return r0, n0, tiles_of(r0, n0), (stored[n0], 32 * r0 + 16)
            return r0, n0, tiles_of(r0, n0), None if fixed(r0, 0) else (stored[n0], 32 * r0)

        @block.vector
        def _(dve):
            def ln1_stats_of(r, n):
                dve.wait_ge(h_ready, group_no(r, n))
                for k in tiles_of(r, n):
                    rows = rows_of(r, k)
                    last = dve.bn_stats(ln1_stats[0:rows, k], h[0:rows, k])
                return last

            def ln1_moments(r, n):
                for k in tiles_of(r, n):
                    rows = rows_of(r, k)
                    last = dve.bn_aggr(ln1_mv[0:rows, k], ln1_stats[0:rows, k])
                return last

            def ln1_add_eps(r, n):
                a, z = tiles_of(r, n)[0], tiles_of(r, n)[-1] + 1
                dve.tensor_scalar(ln1_var[:, a:z], ln1_mv[:, a:z, 1], LN_EPS, None, ALU.add).then_inc(ln1_var_ready, 1)

            def normalise(r, n):
                dve.wait_ge(ln1_rstd_ready, group_no(r, n) + 1)
                for k in tiles_of(r, n):
                    rows = rows_of(r, k)
                    last = dve.tensor_scalar(x_hat[0:rows, k], h[0:rows, k], ln1_mv[0:rows, k, 0:1],
                                             ln1_rstd[0:rows, k:k + 1], ALU.subtract, ALU.mult)
                last.then_inc(x_hat_ready, 1)

            def add_out(r, n, k):
                rows = rows_of(r, k)
                dve.wait_ge(out_done, tile_no(r, k) + 1)
                dve.tensor_tensor(h2[0:rows, k], out_ps[THIRD[k]][0:rows, 0:E], h[0:rows, k],
                                  ALU.add).then_inc(h2_ready, 1)
                dve.wait_ge(h2_ready, tile_no(r, k) + 1)
                last = dve.bn_stats(ln2_stats[0:rows, k], h2[0:rows, k])
                if fixed(r, BODIES) and k == HALF_TILE:
                    last.then_inc(last_stats_ready, 1)

            def low_parts(r, n):
                dve.wait_ge(x_hat_t_ready, group_no(r, n) + 1)
                for k0, count, rows in parts(r, n):
                    last = dve.tensor_tensor(x_parts[:, 1, k0:k0 + count, 0:rows], x_hat_t[:, k0:k0 + count, 0:rows],
                                             x_parts[:, 0, k0:k0 + count, 0:rows], ALU.subtract)
                last.then_inc(x_parts_ready, 1)

            def ln2_moments(r, n, tiles, _):
                for k in tiles:
                    rows = B if fixed(r, -1) else rows_of(r, k)
                    last = dve.bn_aggr(ln2_mv[0:rows, k], ln2_stats[0:rows, k])
                return last

            def ln2_add_eps(r, n, tiles, _):
                a, z, rows = tiles[0], tiles[-1] + 1, B if fixed(r, -1) else P
                dve.tensor_scalar(ln2_var[0:rows, a:z], ln2_mv[0:rows, a:z, 1], LN_EPS, None,
                                  ALU.add).then_inc(ln2_var_ready, 1)

            def ln2_result(r, n, tiles, slots_free):
                group, rows = group_no(r, n), B if fixed(r, -1) else P
                a, z = tiles[0], tiles[-1] + 1
                dve.wait_ge(ln2_rstd_ready, group + 1)
                dve.tensor_scalar(ln2_gain[0:rows, a:z], ln2_rstd[0:rows, a:z], 1.0, None, ALU.add)
                dve.scalar_tensor_tensor(ln2_shift[0:rows, a:z], ln2_mv[0:rows, a:z, 0], -1.0,
                                         ln2_rstd[0:rows, a:z], ALU.mult, ALU.mult).then_inc(ln2_affine_ready, 1)
                dve.wait_ge(ln2_affine_ready, group + 1)
                if slots_free:
                    dve.wait_ge(*slots_free)
                for k in tiles:
                    m = min(rows, rows_of(r, k))
                    last = dve.tensor_scalar(result[0:m, k], h2[0:m, k], ln2_gain[0:m, k:k + 1],
                                             ln2_shift[0:m, k:k + 1], ALU.mult, ALU.add)
                last.then_inc(result_ready, 1)

            def ln2_last_moments(r, n):
                last = before(r, n + 1)
                dve.wait_ge(last_stats_ready, 1)
                ln2_moments(*last).then_inc(mv_ready, 1)
                dve.wait_ge(mv_ready, group_no(r, n) + 5)
                ln2_add_eps(*last)

            def step(r, n):
                tiles, prev = tiles_of(r, n), before(r, n)
                after, second, third = (next_group(r, n, ahead) for ahead in (1, 2, 3))
                if second:
                    normalise(*second)
                if after and in_parts(*after):
                    low_parts(*after)
                if not (fixed(r, 0) and n == 0):
                    ln2_result(*before(*prev[:2]))
                scale_part(dve, VECTOR_SHIFTS, scaled_vector, r, n, 0)
                add_out(r, n, tiles[0])
                if third:
                    ln1_stats_of(*third)
                scale_part(dve, VECTOR_SHIFTS, scaled_vector, r, n, 1)
                add_out(r, n, tiles[1])
                if third:
                    ln1_moments(*third)
                ln2_moments(*prev).then_inc(mv_ready, 1)
                dve.wait_ge(mv_ready, group_no(r, n) + 4)
                if third:
                    ln1_add_eps(*third)
                ln2_add_eps(*prev)
                scale_part(dve, VECTOR_SHIFTS, scaled_vector, r, n, 2)
                for k in tiles[2:]:
                    add_out(r, n, k)
                if not after:
                    ln2_last_moments(r, n)
                    ln2_result(*prev)

            dve.memset(offset_rows[:, :, 0], 0.0)
            dve.memset(offset_rows[:, :, N], 0.0)
            dve.memset(offset_rows[0:B, 0, 1:N], 0.0).then_inc(pads_ready, 1)
            dve.memset(scale_cols[:], 0.0).then_inc(cols_zero, 1)
            dve.wait_ge(cls_in, 16)
            dve.bn_stats(ln1_stats[0:B, CLS], h[0:B, CLS]).then_inc(cls_stats_ready, 1)
            dve.wait_ge(cls_stats_ready, 1)
            dve.bn_aggr(ln1_mv[0:B, CLS], ln1_stats[0:B, CLS]).then_inc(mv_ready, 1)
            dve.wait_ge(mv_ready, 1)
            dve.tensor_scalar(ln1_var[0:B, CLS:CLS + 1], ln1_mv[0:B, CLS, 1:2], LN_EPS, None,
                              ALU.add).then_inc(ln1_var_ready, 1)
            dve.wait_ge(gamma_in, 16)
            dve.wait_ge(patch_in[0], 16)
            dve.wait_ge(first_offsets_in, 16 * 6)
            for s in range(3):
                last = scale_shift(dve, s, 0, 0)
            last.then_inc(scaled_vector, 1)
            dve.wait_ge(ln1_rstd_ready, 1)
            dve.tensor_scalar(x_hat[0:B, CLS], h[0:B, CLS], ln1_mv[0:B, CLS, 0:1],
                              ln1_rstd[0:B, CLS:CLS + 1], ALU.subtract, ALU.mult).then_inc(x_hat_ready, 1)
            for i, (row, rows) in enumerate(STAT_CHUNKS):
                dve.wait_ge(images_in[i], 16)
                for j, (first, count, cols, _) in enumerate(STATS):
                    if row <= first + count - 1 < row + rows:
                        part = images[:, first:first + count]
                        if cols == "mid":
                            part = part[:, :, HALF:S - HALF]
                        else:
                            part = part.rearrange("p r (g q) -> p r g q", q=HALF)[:, :, 0:S // HALF:S // HALF - 1]
                        last_stats = dve.bn_stats(stats[:, 2 * j:2 * j + 2].rearrange("p a b -> p (a b)"), part)
                if i == 1:
                    dve.wait_ge(patch_in[1], 16)
                    scale_shift(dve, 0, 1, 1).then_inc(scaled_vector, 1)
            last_stats.then_inc(stats_step, 1)
            dve.wait_ge(stats_step, 1)
            dve.wait_ge(consts_ready, 1)
            dve.tensor_tensor(stat_tmp[:, 0], stats[:, :, 1], stat_w[:, 0], ALU.mult)
            dve.tensor_tensor(stat_tmp[:, 2], stats[:, :, 2], stat_w[:, 1], ALU.mult).then_inc(stats_step, 1)
            dve.wait_ge(stats_step, 2)
            dve.tensor_reduce(sums[:, 0:1], stat_tmp[:, 0], AX.X, ALU.add).then_inc(sums_ready, 1)
            dve.tensor_tensor(stat_tmp[:, 1], stat_tmp[:, 0], stats[:, :, 1], ALU.mult).then_inc(stats_step, 1)
            dve.wait_ge(stats_step, 3)
            dve.tensor_tensor(stat_tmp[:, 0], stat_tmp[:, 1], stat_tmp[:, 2], ALU.add).then_inc(stats_step, 1)
            dve.wait_ge(stats_step, 4)
            dve.tensor_reduce(sums[:, 1:2], stat_tmp[:, 0], AX.X, ALU.add).then_inc(sums_ready, 1)
            dve.wait_ge(image_sums_done, 1)
            dve.tensor_scalar(moments[:, 0:2], out_ps[2][:, 0:2], 1.0 / PIXELS, None, ALU.mult).then_inc(stats_step, 1)
            dve.wait_ge(stats_step, 5)
            dve.tensor_tensor(moments[:, 2:3], moments[:, 0:1], moments[:, 0:1], ALU.mult).then_inc(stats_step, 1)
            dve.wait_ge(stats_step, 6)
            dve.scalar_tensor_tensor(moments[:, 3:4], moments[:, 1:2], TOK_EPS, moments[:, 2:3], ALU.add,
                                     ALU.subtract).then_inc(image_var_ready, 1)
            dve.wait_ge(cols_zero, 1)
            for half in range(2):
                a = half * B
                dve.tensor_scalar(scale_cols[a:a + B, half, 1:2], moments[a:a + B, 0:1], -1.0, None,
                                  ALU.mult).then_inc(cols_ready, 1)
            dve.wait_ge(image_scale_ready, 1)
            for half in range(2):
                a = half * B
                dve.tensor_copy(scale_cols[a:a + B, half, 0:1], moments[a:a + B, 4:5]).then_inc(cols_ready, 1)
            def once_each(cols):
                return cols.unsqueeze(2).to_broadcast([P, 2, PARTS, 2])

            dve.wait_ge(cols_ready, 4)
            dve.tensor_copy(scale_parts[:, :, 0], once_each(scale_cols[:])).then_inc(scale_parts_ready, 1)
            dve.wait_ge(scale_parts_ready, 1)
            dve.tensor_tensor(scale_rest[:], scale_cols[:], scale_parts[:, :, 0, 0],
                              ALU.subtract).then_inc(scale_rest_ready, 1)
            dve.wait_ge(scale_rest_ready, 1)
            dve.tensor_copy(scale_parts[:, :, 1], once_each(scale_rest[:])).then_inc(scale_parts_ready, 1)
            dve.wait_ge(scale_parts_ready, 2)
            dve.tensor_tensor(scale_parts[:, :, 2], once_each(scale_rest[:]), scale_parts[:, :, 1],
                              ALU.subtract).then_inc(scale_parts_ready, 1)
            dve.wait_ge(out_done, 1)
            dve.tensor_tensor(h2[0:B, CLS], out_ps[THIRD[CLS]][0:B, 0:E], h[0:B, CLS],
                              ALU.add).then_inc(h2_ready, 1)
            dve.wait_ge(h2_ready, 1)
            dve.bn_stats(ln2_stats[0:B, CLS], h2[0:B, CLS])
            dve.wait_ge(patch_in[0], 32)
            dve.wait_ge(conv_done, 2)
            for s in range(2):
                last = scale_shift(dve, s, 2, 0)
            last.then_inc(scaled_vector, 1)
            def first_h(n):
                k0, z = GROUPS[n][0], GROUPS[n][-1] + 1
                dve.wait_ge(h_ready, n + 1)
                dve.scalar_tensor_tensor(h[:, k0:z], result[:, k0:z], moments[:, 5:6], h[:, k0:z], ALU.mult,
                                         ALU.add).then_inc(first_h_ready, 1)

            def first_moments(n):
                if n < 2:
                    dve.wait_ge(first_h_ready, n + 1)
                ln1_stats_of(0, n).then_inc(first_stats_ready, 1)
                dve.wait_ge(first_stats_ready, n + 1)
                ln1_moments(0, n).then_inc(mv_ready, 1)
                dve.wait_ge(mv_ready, n + 2)
                ln1_add_eps(0, n)

            first_h(0)
            first_moments(0)
            first_h(1)
            normalise(0, 0)
            first_moments(1)
            first_moments(2)
            normalise(0, 1)
            for n in range(NG):
                step(0, n)
            with dve.Fori(1, BODIES - 2) as r:
                for n in range(NG):
                    step(r, n)
            for r in (BODIES - 2, BODIES - 1):
                for n in range(NG):
                    step(r, n)
            for n in range(len(TAIL_GROUPS)):
                step(BODIES, n)
            ln2_result(*before(BODIES, len(TAIL_GROUPS)))

        @block.gpsimd
        def _(pool):
            def ln1_power(r, n):
                a, z = tiles_of(r, n)[0], tiles_of(r, n)[-1] + 1
                pool.wait_ge(ln1_var_ready, group_no(r, n) + 1)
                pool.tensor_tensor(ln1_rstd[:, a:z], ln1_var[:, a:z], powers[:, 1:1 + z - a],
                                   ALU.pow).then_inc(ln1_rstd_ready, 1)

            def ln2_power(r, n, tiles, _):
                a, z, rows = tiles[0], tiles[-1] + 1, B if fixed(r, -1) else P
                pool.wait_ge(ln2_var_ready, group_no(r, n) + 1)
                pool.tensor_tensor(ln2_rstd[0:rows, a:z], ln2_var[0:rows, a:z], powers[0:rows, 1:1 + z - a],
                                   ALU.pow).then_inc(ln2_rstd_ready, 1)

            def step(r, n):
                third = next_group(r, n, 3)
                scale_part(pool, POOL_SHIFTS, scaled_pool, r, n, 0)
                if third:
                    ln1_power(*third)
                ln2_power(*before(r, n))
                scale_part(pool, POOL_SHIFTS, scaled_pool, r, n, 1)

            pool.memset(bias_row[:], 0.0).then_inc(bias_zero, 1)
            pool.memset(powers[:, 1:5], -0.5)
            pool.memset(powers[:, 0:1], 0.5)
            pool.memset(ones[:], 1.0)
            pool.memset(terms[:, PATCHES // 2], 0.0)
            for a, z in ((0, 2), (2, 4), (4, 6), (6, len(STATS))):
                _, rows, cols, w = STATS[a]
                count = rows * (S - 2 * HALF if cols == "mid" else 2 * HALF)
                pool.memset(stat_w[:, 0, 2 * a:2 * z], float(w * count // 2))
                last = pool.memset(stat_w[:, 1, 2 * a:2 * z], float(w))
            last.then_inc(consts_ready, 1)
            pool.wait_ge(consts_ready, 1)
            pool.wait_ge(ln1_var_ready, 1)
            pool.tensor_tensor(ln1_rstd[0:B, CLS:CLS + 1], ln1_var[0:B, CLS:CLS + 1], powers[0:B, 1:2],
                               ALU.pow).then_inc(ln1_rstd_ready, 1)
            pool.wait_ge(gamma_in, 16)
            pool.wait_ge(first_offsets_in, 16 * 6)
            for s in (3, 4):
                last = scale_shift(pool, s, 0, 0)
            last.then_inc(scaled_pool, 1)
            for blk in range(2):
                m = P if blk == 0 else PATCHES - P
                parts_of, rest = term_parts[0:m, blk], term_rest[0:m, blk]
                pool.wait_ge(term_rows_ready, blk + 1)
                pool.tensor_copy(parts_of[:, 0], term_rows[0:m, blk]).then_inc(term_step, 1)
                pool.wait_ge(term_step, 3 * blk + 1)
                pool.tensor_tensor(rest, term_rows[0:m, blk], parts_of[:, 0], ALU.subtract).then_inc(term_step, 1)
                pool.wait_ge(term_step, 3 * blk + 2)
                pool.tensor_copy(parts_of[:, 1], rest).then_inc(term_step, 1)
                pool.wait_ge(term_step, 3 * blk + 3)
                pool.tensor_tensor(parts_of[:, 2], rest, parts_of[:, 1], ALU.subtract).then_inc(term_parts_ready, 1)
            pool.wait_ge(offset_in[0], 64)
            for s in (1, 2, 3, 4):
                last = scale_shift(pool, s, 1, 1)
            last.then_inc(scaled_pool, 1)
            pool.wait_ge(w_vr_ready, 2)
            pool.tensor_copy(w_parts[:, 0], w_vr[:]).then_inc(w_high_ready, 1)
            pool.wait_ge(w_high_ready, 1)
            pool.tensor_tensor(w_parts[:, 1], w_vr[:], w_parts[:, 0], ALU.subtract).then_inc(w_parts_ready, 1)
            pool.wait_ge(conv_done, 2)
            for s in (3, 4):
                scale_shift(pool, s, 2, 0)
            pool.wait_ge(image_var_ready, 1)
            pool.tensor_tensor(moments[:, 4:6], moments[:, 3:4].to_broadcast([P, 2]), powers[:, 0:2],
                               ALU.pow).then_inc(image_scale_ready, 1)
            pool.wait_ge(offset_in[1], 64)
            scale_shift(pool, 2, 2, 0).then_inc(scaled_pool, 1)
            for n in range(3):
                ln1_power(0, n)
            for n in range(NG):
                step(0, n)
            with pool.Fori(1, BODIES - 2) as r:
                for n in range(NG):
                    step(r, n)
            pool.wait_ge(scaled_vector, 2 * (BODIES - 1))
            pool.wait_ge(scaled_pool, 2 * (BODIES - 1) + 1)
            pool.wait_ge(ln2_rstd_ready, group_no(BODIES - 3, NG - 2) + 1)
            pool.memset(offset_rows[B:P, 1], 0.0).then_inc(last_pad, 1)
            pool.wait_ge(last_pad, 1)
            for r in (BODIES - 2, BODIES - 1):
                for n in range(NG):
                    step(r, n)
            for n in range(len(TAIL_GROUPS)):
                step(BODIES, n)
            ln2_power(*before(BODIES, len(TAIL_GROUPS)))


def kernel(x, cls_tok, L0_tok_gamma, L0_tok_beta, L0_tok_W, L0_tok_b, L0_attn_Wq, L0_attn_Wk, L0_attn_Wv,
           L0_attn_memory0, L0_ffn_W, L0_ffn_b):
    import numpy as np
    import concourse.bacc as bacc
    from concourse.bass_utils import run_bass_kernel_spmd

    def windows(a):
        m = a.shape[0]
        a = a.reshape(m, 2, N, 2, HALF, N, 2, HALF)
        return a.transpose(3, 6, 1, 4, 7, 0, 2, 5).reshape(P, m, N, N)

    x, gamma, beta, w = (np.asarray(a) for a in (x, L0_tok_gamma, L0_tok_beta, L0_tok_W))
    arrays = {
        "x_rows": x.reshape(P, S, S),
        "x_win": windows(x).transpose(0, 2, 3, 1),
        "gamma": windows(gamma.reshape(SHIFTS, 2, S, S)).reshape(P, SHIFTS, PATCHES),
        "beta": windows(beta.reshape(SHIFTS, 2, S, S)).reshape(P, SHIFTS, PATCHES),
        "weight": w.reshape(E, SHIFTS, 2, 2, HALF, 2, HALF).transpose(3, 5, 2, 4, 6, 1, 0).reshape(P, SHIFTS, E),
        "bias": np.asarray(L0_tok_b).reshape(1, E),
        "cls_tok": np.asarray(cls_tok).reshape(E),
        "wq": np.asarray(L0_attn_Wq),
        "wk": np.asarray(L0_attn_Wk),
        "wv_t": np.asarray(L0_attn_Wv).T,
        "mem_t": np.asarray(L0_attn_memory0).T,
        "ident": np.eye(P, dtype=np.float32),
        "same_image": np.kron(np.eye(B, dtype=np.float32), np.ones((2, 1), np.float32))[:, list(range(B)) * 2],
    }
    nc = bacc.Bacc("TRN2", target_bir_lowering=False, num_devices=1)
    in_map, args = {}, []
    for name, a in arrays.items():
        in_map[name] = np.ascontiguousarray(a)
        args.append(nc.dram_tensor(name, in_map[name].shape, F32, kind="ExternalInput").ap())
    args.append(nc.dram_tensor("out", (B, PATCHES + 1, E), F32, kind="ExternalOutput").ap())
    args.append(nc.dram_tensor("parked", (2, 2 * PARTS, PATCHES // 2 + 1, E), BF16, kind="Internal").ap())
    tower(nc, *args)
    return run_bass_kernel_spmd(nc, [in_map], core_ids=[0]).results[0]["out"]
```
